# Optimizing a Trainium2 kernel written in Bass

```python
import numpy as np
import jax
import jax.numpy as jnp

def _softmax(x, axis=-1):
    return jax.nn.softmax(x, axis=axis)

def _gelu(x):
    return jax.nn.gelu(x, approximate=True)

def _silu(x):
    return jax.nn.silu(x)

def _sigmoid(x):
    return jax.nn.sigmoid(x)

def _layernorm(x, axis=-1, eps=1e-05):
    m = jnp.mean(x, axis=axis, keepdims=True)
    v = jnp.var(x, axis=axis, keepdims=True)
    return (x - m) / jnp.sqrt(v + eps)

def _scatter_add(tgt, idx, src, axis=0):
    return tgt.at[idx].add(src)

def _segment_sum(src, seg, n):
    return jax.ops.segment_sum(src, seg, n)
kernel_name = 'mk_gnn_resnorm_d2_gnn_r16_fe69d6'

def setup_inputs(seed: int=0):
    np.random.seed(seed)
    _w = jnp.asarray

    def _rec_inputs():
        import jax
        import jax.numpy as jnp
        _gk = jax.random.key(seed)
        x = -0.0004402 + 1 * jax.random.normal(jax.random.fold_in(_gk, 1), (6250, 16), jnp.float32)
        src = jax.random.randint(jax.random.fold_in(_gk, 2), (200000,), 0, 6250, jnp.int32)
        dst = jax.random.randint(jax.random.fold_in(_gk, 3), (200000,), 0, 6250, jnp.int32)
        _o = jnp.argsort(dst, stable=True)
        src = src[_o]
        dst = dst[_o]
        edge_attr_16 = -3.57403e-05 + 0.999761 * jax.random.normal(jax.random.fold_in(_gk, 12), (200000, 16), jnp.float32)
        return (x, src, dst, edge_attr_16)
    x, src, dst, edge_attr_16 = _rec_inputs()

    def _L0_gnn_setup():
        import jax, jax.numpy as jnp
        import numpy as np
        N_NODES = 1875
        N_EDGES = 18750
        IN_FEATS = 16
        OUT_FEATS = 16
        EDGE_DIM = 16
        key = jax.random.key(seed)
        ks = jax.random.split(key, 8)
        feat = jax.random.normal(ks[0], (N_NODES, IN_FEATS), dtype=jnp.float32)
        efeat = jax.random.normal(ks[1], (N_EDGES, EDGE_DIM), dtype=jnp.float32)
        W_msg = jax.random.normal(ks[2], (EDGE_DIM, IN_FEATS * OUT_FEATS), dtype=jnp.float32) * 0.1
        b_msg = jnp.zeros((IN_FEATS * OUT_FEATS,), dtype=jnp.float32)
        W_attn = jax.random.normal(ks[3], (EDGE_DIM, IN_FEATS * OUT_FEATS), dtype=jnp.float32) * 0.1
        b_attn = jnp.zeros((IN_FEATS * OUT_FEATS,), dtype=jnp.float32)
        src = jax.random.randint(ks[4], (N_EDGES,), 0, N_NODES, dtype=jnp.int32)
        dst = jax.random.randint(ks[5], (N_EDGES,), 0, N_NODES, dtype=jnp.int32)
        return {'feat': feat, 'efeat': efeat, 'W_msg': W_msg, 'b_msg': b_msg, 'W_attn': W_attn, 'b_attn': b_attn, 'src': src, 'dst': dst}
    _L0_gnn_all = _L0_gnn_setup()
    _L0_gnn_in = {k: v for k, v in _L0_gnn_all.items() if k in ('W_msg', 'b_msg', 'W_attn', 'b_attn')}
    del _L0_gnn_all

    def _L1_gnn_setup():
        import jax, jax.numpy as jnp
        import numpy as np
        N_NODES = 6250
        N_EDGES = 200000
        D_FEAT = 16
        key = jax.random.key(seed)
        k1, k2, k3 = jax.random.split(key, 3)
        x = jax.random.normal(k1, (N_NODES, D_FEAT), dtype=jnp.float32)
        edge_index = jax.random.randint(k2, (2, N_EDGES), 0, N_NODES, dtype=jnp.int64)
        edge_attr = jax.random.normal(k3, (N_EDGES, D_FEAT), dtype=jnp.float32)
        return {'x': x, 'edge_index': edge_index, 'edge_attr': edge_attr}
    _L1_gnn_all = _L1_gnn_setup()
    _L1_gnn_in = {k: v for k, v in _L1_gnn_all.items() if k in ()}
    del _L1_gnn_all
    return {'x': x, 'src': src, 'dst': dst, 'edge_attr_16': edge_attr_16, 'L0_gnn_W_msg': _L0_gnn_in['W_msg'], 'L0_gnn_b_msg': _L0_gnn_in['b_msg'], 'L0_gnn_W_attn': _L0_gnn_in['W_attn'], 'L0_gnn_b_attn': _L0_gnn_in['b_attn']}

def reference(x, src, dst, edge_attr_16, L0_gnn_W_msg, L0_gnn_b_msg, L0_gnn_W_attn, L0_gnn_b_attn):
    import jax
    import jax.numpy as jnp

    def _L0_gnn_ref(feat, efeat, W_msg, b_msg, W_attn, b_attn, src, dst):
        import jax, jax.numpy as jnp
        import numpy as np
        N_NODES = 1875
        N_EDGES = 18750
        IN_FEATS = 16
        OUT_FEATS = 16
        EDGE_DIM = 16
        N, in_f = feat.shape
        E = efeat.shape[0]
        w_m = (efeat @ W_msg + b_msg).reshape(E, in_f, -1)
        w_a = (efeat @ W_attn + b_attn).reshape(E, in_f, -1)
        h_src = feat[src][:, :, None]
        e1 = w_m * h_src
        e2 = w_a * h_src
        seg_max = jax.ops.segment_max(e2, dst, num_segments=N)
        ex = jnp.exp(e2 - seg_max[dst])
        denom = jax.ops.segment_sum(ex, dst, num_segments=N)
        attn = ex / denom[dst]
        ft = jax.ops.segment_sum(e1 * attn, dst, num_segments=N)
        return ft.sum(axis=1)

    def _L1_gnn_ref(x, edge_index, edge_attr):
        import jax, jax.numpy as jnp
        import numpy as np
        N_NODES = 6250
        N_EDGES = 200000
        D_FEAT = 16
        nb_node = x.shape[0]
        dst = edge_index[1]
        sums = jax.ops.segment_sum(edge_attr, dst, num_segments=nb_node)
        counts = jax.ops.segment_sum(jnp.ones((edge_attr.shape[0],), dtype=edge_attr.dtype), dst, num_segments=nb_node)
        denom = jnp.where(counts > 0, counts, jnp.ones_like(counts))
        return sums / denom[:, None]
    edge_index = jnp.stack([src, dst])
    x = _layernorm(x + _L0_gnn_ref(x, edge_attr_16, L0_gnn_W_msg, L0_gnn_b_msg, L0_gnn_W_attn, L0_gnn_b_attn, src, dst), axis=-1)
    x = _layernorm(x + _L1_gnn_ref(x, edge_index, edge_attr_16), axis=-1)
    return x

_drawn_inputs = setup_inputs


def setup_inputs(seed=0):
    import zlib

    import numpy as np

    out = dict(_drawn_inputs(seed))
    spreads = {'L0_gnn_b_msg': (0.0, 0.1), 'L0_gnn_b_attn': (0.0, 0.1)}
    factors = {}
    for name, (base, spread) in spreads.items():
        noise = np.random.default_rng([zlib.crc32(name.encode()), seed]).standard_normal(out[name].shape)
        drawn = base * np.exp(spread * noise) if base else spread * noise
        out[name] = jnp.asarray(drawn.astype(out[name].dtype))
    for name, factor in factors.items():
        out[name] = (out[name] * factor).astype(out[name].dtype)
    return out
```

```python
import concourse.bass as bass
from concourse import mybir
from contextlib import ExitStack

N = 6250
E = 200000
L = 8
NC = 49
NP = 128 * NC
EB = 512
NB = 391
EC = 1563
EP = 128 * EC
NT = 239
RC = 240
NR = 128 * RC
RW = 41
DW = 528
K = 100
BIG = -1.0e35
NONE = 100000.0
PADS = -1.0e25


def gnn_kernel(nc, xt, dst, src, ea, wc, cst, out):
    f32, bf16, i32 = mybir.dt.float32, mybir.dt.bfloat16, mybir.dt.int32
    ALU, ACT, AX = mybir.AluOpType, mybir.ActivationFunctionType, mybir.AxisListType
    RECD = nc.dram_tensor("rec_d", [EP, RW], i32, kind="Internal").ap()
    RTD = nc.dram_tensor("rt_d", [NR, 4], f32, kind="Internal").ap()
    NIDD = nc.dram_tensor("nid_d", [NR + 2], f32, kind="Internal").ap()
    E0D = nc.dram_tensor("e0_d", [NR], f32, kind="Internal").ap()
    CND = nc.dram_tensor("cn_d", [NR], f32, kind="Internal").ap()
    MKD = nc.dram_tensor("mk_d", [RC, 384], f32, kind="Internal").ap()
    DTD = nc.dram_tensor("dt_d", [NP, DW], f32, kind="Internal").ap()

    ctx = ExitStack()
    with ctx:
        def sb(name, shape, dt=f32):
            return ctx.enter_context(nc.sbuf_tensor(name, shape, dt))

        def sem(name):
            return ctx.enter_context(nc.semaphore(name))

        CS = sb("CS", [128, 692])
        IDN, TRI, E127 = CS[:, 0:128], CS[:, 128:256], CS[:, 256:257]
        NVAL, RID, IO8 = CS[:, 257:307], CS[:, 307:547], CS[:, 547:555]
        SENT, ONE = CS[0:1, 555:557], CS[0:1, 557:685]
        IDB = sb("IDB", [128, 128], bf16)
        FI = sb("FI", [1, NB], i32)
        FF = sb("FF", [1, NB])
        FB = sb("FB", [128, NB])
        JK = sb("JK", [128, 512])
        BC = sb("BC", [128, 50])
        QF = sb("QF", [128, 50])
        QI = sb("QI", [128, 50], i32)
        EM = sb("EM", [128, 3, L * 512])
        BL = EM[:, 1, 0:4 * EB].bitcast(i32).rearrange("p (b e) -> p b e", b=4)
        BF = EM[:, 1, 4 * EB:8 * EB].rearrange("p (b e) -> p b e", b=4)
        CB = sb("CB", [128, 50])
        SS = sb("SS", [128, 50])
        DG = sb("DG", [128, NC])
        T1 = sb("T1", [128, NC])
        TI = sb("TI", [128, NC], i32)
        TJ = sb("TJ", [128, NC], i32)
        NRW = sb("NRW", [128, NC])
        INC = sb("INC", [128, NC])
        OFF = sb("OFF", [128, 1])
        NV = sb("NV", [128, NC, 4])
        SI = sb("SI", [128, NC], i32)
        ZR = sb("ZR", [128, RC])
        M1 = EM[:, 2, 0:960]
        RT = EM[:, 2, 960:1920].rearrange("p (c w) -> p c w", w=4)
        F4 = EM[:, 2, 1920:2880].rearrange("p (w c) -> p w c", w=4)
        F5 = EM[:, 2, 2880:3840].rearrange("p (w c) -> p w c", w=4)
        CX = sb("CX", [4, 132])
        CT = sb("CT", [4, 128])
        CY = sb("CY", [128, 4])
        R1 = sb("R1", [128, RC])
        R2 = sb("R2", [128, RC])
        R3 = sb("R3", [128, RC])
        RE = sb("RE", [128, RC])
        RCN = sb("RCN", [128, RC])
        RN = sb("RN", [128, RC])
        TN = sb("TN", [120, 2, 130])
        TE = sb("TE", [120, 2, 128])
        TC = sb("TC", [120, 2, 128])
        TS = sb("TS", [120, 2, 128])
        MKT = sb("MKT", [120, 2, 384])
        NID = sb("NID", [128, RC])
        E0 = sb("E0", [128, RC], i32)
        CNT = sb("CNT", [128, RC])
        SX = sb("SX", [128, RC], i32)
        INV = EM[:, 0, 2176:4096].rearrange("p (c j) -> p c j", j=L)
        VAL = sb("VAL", [128, RC, L])
        INI = sb("INI", [128, RC, L], i32)
        FLG = sb("FLG", [128, RC, L], bf16)
        DI = sb("DI", [128, DW])
        WF = sb("WF", [17, 512])
        WH = sb("WH", [17, 3, 512], bf16)
        WD = sb("WD", [17, 512])
        FLW = sb("FLW", [1, 512], bf16)
        WS = sb("WS", [K, 512], bf16)
        CH = 66
        chunks = [(o, min(CH, EC - o)) for o in range(0, EC, CH)]
        XI = EM[:, 0, 0:2 * CH * 16].rearrange("p (b c k) -> p b c k", b=2, k=16)
        SR = sb("SR", [128, EC], i32)
        XD = EM[:, 0, 2 * CH * 16:3 * CH * 16].rearrange("p (c k) -> p c k", k=16)
        RB = sb("RB", [128, 2, CH, RW], i32)
        REC = sb("REC", [128, 3, L * RW], i32)
        IX = sb("IX", [128, 3, L], i32)
        H = sb("H", [128, 3, L * 16])
        XP = sb("XP", [128, 2, L, K], bf16)
        LT = sb("LT", [K, 2, L * 128], bf16)
        MX = sb("MX", [128, 256])
        MF = sb("MF", [128, 256])
        MT = sb("MT", [128, 2, 256])
        MK = sb("MK", [128, 3, 384])
        U = sb("U", [128, 3, 128])
        SEL = sb("SEL", [128, 3, 128])
        DL = sb("DL", [128, 2])
        DR = sb("DR", [128, 2])
        AL = sb("AL", [128, 2])
        DNS = sb("DNS", [128, 4, DW])
        DSC = sb("DSC", [128, 512])
        EV = sb("EV", [128, L, 16])
        EA = sb("EA", [128, 4, 16])
        EB2 = sb("EB2", [128, 2, 16])
        ES = sb("ES", [128, 2, 16])
        DTT = EM[:, 0, 0:4 * DW].rearrange("p (b w) -> p b w", w=DW)
        RCP = sb("RCP", [128, 256])
        PRD = sb("PRD", [128, 256])
        FT = sb("FT", [128, NC, 16])
        SA = sb("SA", [128, NC, 16])
        XN = sb("XN", [128, NC, 16])
        Y = sb("Y", [128, NC, 16])
        Y2 = sb("Y2", [128, NC, 16])
        ST = sb("ST", [128, 4, NC])
        RCN2 = sb("RCN2", [128, NC])

        PW = ctx.enter_context(nc.psum_tensor("PW", [128, 4, 512], f32))
        PTB = ctx.enter_context(nc.psum_tensor("PTB", [128, L * 128], bf16))
        PMB = ctx.enter_context(nc.psum_tensor("PMB", [128, 512], f32))
        PDN = ctx.enter_context(nc.psum_tensor("PDN", [128, 512], f32))
        PAL = ctx.enter_context(nc.psum_tensor("PAL", [128, 512], f32))

        names = """d_cs d_f d_w d_w2 d_sr d_i0 d_i1 d_sc0 d_rl d_s1 d_tl d_mkd d_out d_xn
            v_id v_p v_pc v_q v_blk v_rr v_tr v_rb v_w v_x1 v_x3
            v_mult v_rmax v_u v_scan v_del v_sev v_gm v_cm v_sub v_e v_var v_fin
            p_f p_o p_x p_y p_t p_T p_W p_mT p_S p_MB p_al p_sum
            a_w a_blk a_x0 a_x2 a_xp a_T a_exp a_rel a_al a_dn a_z a_sa
            g_m g_idx g_ev""".split()
        S = {n: sem(n) for n in names}
        d_xi = [sem(f"d_xi{i}") for i in range(2)]
        d_ro = [sem(f"d_ro{i}") for i in range(2)]
        d_bl = [sem(f"d_bl{i}") for i in range(4)]
        d_rec = [sem(f"d_rec{i}") for i in range(3)]
        d_h = [sem(f"d_h{i}") for i in range(3)]
        d_mk = [sem(f"d_mk{i}") for i in range(3)]
        d_st = [sem(f"d_st{i}") for i in range(4)]
        d_dt = [sem(f"d_dt{i}") for i in range(4)]
        nq = len(chunks)

        block = ctx.enter_context(nc.Block())

        @block.sync
        def _(sp):
            sp.dma_start(CS[:, :], cst).then_inc(S["d_cs"], 16)
            sp.dma_start(FI[:, :], dst.rearrange("(b e) -> e b", e=EB)[0:1, :],
                         allow_slow_non_contiguous=True).then_inc(S["d_f"], 16)
            sp.dma_start(WF[:, :], wc).then_inc(S["d_w"], 16)
            sp.dma_start(SR[:, :], src.rearrange("(p c) -> p c", c=EC)).then_inc(S["d_sr"], 16)
            eav = ea.rearrange("(p c) k -> p c k", c=EC)
            recv = RECD.rearrange("(p c) w -> p c w", c=EC)

            def load(q):
                o, n = chunks[q]
                if q >= 2:
                    sp.wait_ge(S["a_x0"], 4 * (q - 2) + 4)
                    sp.wait_ge(S["v_x1"], q - 1)
                sp.dma_start(XI[:, q % 2, 0:n, :], eav[:, o:o + n, :]).then_inc(d_xi[q % 2], 16)

            load(0)
            load(1)
            for q, (o, n) in enumerate(chunks):
                sp.wait_ge(S["a_x0"], 4 * q + 4)
                sp.wait_ge(S["v_x3"], q + 1)
                sp.dma_start(recv[:, o:o + n, :], RB[:, q % 2, 0:n, :]).then_inc(d_ro[q % 2], 16)
                if q == 0:
                    sp.wait_ge(S["a_w"], 2)
                    sp.wait_ge(S["v_w"], 2)
                    sp.wait_ge(S["g_m"], 5)
                    for k, part in enumerate((0, 0, 0, 1, 1, 2)):
                        sp.dma_start(WS[16 * k:16 * k + 16, :], WH[0:16, part, :]).then_inc(S["d_w2"], 16)
                    for k in range(3):
                        sp.dma_start(WS[96 + k:97 + k, :], WH[16:17, k, :]).then_inc(S["d_w2"], 16)
                    sp.dma_start(WS[99:100, :], FLW[:, :]).then_inc(S["d_w2"], 16)
                    sp.wait_ge(S["g_m"], 8)
                    sp.dma_start(RTD.rearrange("(p c) w -> p (c w)", c=RC), M1[:, :]).then_inc(S["d_i0"], 16)
                    for c in range(NC):
                        sp.dma_start(DTD[128 * c:128 * c + 128, :], DI[:, :]).then_inc(S["d_i1"], 16)
                if q + 2 < nq:
                    load(q + 2)
            sp.wait_ge(S["d_sc0"], 16 * NC)
            sp.dma_start(RT[:, :, :], RTD.rearrange("(p c) w -> p c w", c=RC)).then_inc(S["d_rl"], 16)
            sp.wait_ge(S["v_rr"], 3)
            sp.dma_start(E0D.rearrange("(p c) -> p c", c=RC), RE[:, :]).then_inc(S["d_s1"], 16)
            sp.dma_start(CND.rearrange("(p c) -> p c", c=RC), RCN[:, :]).then_inc(S["d_s1"], 16)
            sp.dma_start(NIDD[1:NR + 1].rearrange("(p c) -> p c", c=RC), RN[:, :]).then_inc(S["d_s1"], 16)
            sp.dma_start(NIDD[0:1].unsqueeze(0), SENT[:, 0:1]).then_inc(S["d_s1"], 16)
            sp.dma_start(NIDD[NR + 1:NR + 2].unsqueeze(0), SENT[:, 1:2]).then_inc(S["d_s1"], 16)
            sp.wait_ge(S["d_s1"], 80)
            v0 = NIDD[0:NR].rearrange("(h t r) -> t h r", h=2, r=128)
            v1 = NIDD[2:NR + 2].rearrange("(h t r) -> t h r", h=2, r=128)
            sp.dma_start(TN[:, :, 0:128], v0).then_inc(S["d_tl"], 16)
            sp.dma_start(TN[:, :, 128:130], v1[:, :, 126:128]).then_inc(S["d_tl"], 16)
            sp.dma_start(TE[:, :, :], E0D.rearrange("(h t r) -> t h r", h=2, r=128)).then_inc(S["d_tl"], 16)
            sp.dma_start(TC[:, :, :], CND.rearrange("(h t r) -> t h r", h=2, r=128)).then_inc(S["d_tl"], 16)
            sp.wait_ge(S["v_tr"], 6)
            sp.dma_start(MKD.rearrange("(h t) r -> t h r", h=2), MKT[:, :, :]).then_inc(S["d_mkd"], 16)
            sp.wait_ge(S["d_mkd"], 16)
            sp.dma_start(XN[:, :, :], xt[0:NP, :].rearrange("(p c) k -> p c k", c=NC)).then_inc(S["d_xn"], 16)
            for t in range(NT):
                if t >= 3:
                    sp.wait_ge(S["v_scan"], 4 * (t - 3) + 4)
                    sp.wait_ge(S["v_u"], 2 * (t - 3) + 2)
                sp.dma_start(MK[:, t % 3, :], MKD[t:t + 1, :].broadcast_to([128, 384])).then_inc(d_mk[t % 3], 16)
            for b in range(4):
                sp.wait_ge(d_st[b], 16 * len(range(b, NT, 4)))
            dtv = DTD.rearrange("(p c) w -> p c w", c=NC)
            for c in range(NC):
                if c >= 4:
                    sp.wait_ge(S["v_e"], 3 * (c - 4) + 2)
                    sp.wait_ge(S["a_sa"], c - 3)
                sp.dma_start(DTT[:, c % 4, :], dtv[:, c, :]).then_inc(d_dt[c % 4], 16)
            sp.wait_ge(S["v_fin"], 1)
            sp.dma_start(out[0:127 * NC, :].rearrange("(p c) k -> p c k", c=NC), Y2[0:127, :, :]).then_inc(S["d_out"], 16)
            sp.dma_start(out[127 * NC:N, :].unsqueeze(0), Y2[127:128, 0:N - 127 * NC, :]).then_inc(S["d_out"], 16)
            sp.wait_ge(S["d_out"], 32)

        @block.gpsimd
        def _(g):
            g.memset(FLW[:, :], 0.0).then_inc(S["g_m"], 1)
            g.wait_ge(S["g_m"], 1)
            flv = FLW[:, :].rearrange("p (i a o) -> p i a o", a=2, o=16)
            g.memset(M1[:, :], -1.0).then_inc(S["g_m"], 1)
            g.memset(DI[:, :], 0.0).then_inc(S["g_m"], 1)
            g.wait_ge(S["g_m"], 3)
            div = DI[:, 0:512].rearrange("p (i a o) -> p i a o", a=2, o=16)
            g.memset(div[:, :, 0, :], 1.0).then_inc(S["g_m"], 1)
            g.memset(flv[:, :, 0, :], PADS).then_inc(S["g_m"], 1)
            g.memset(ZR[:, :], 0.0).then_inc(S["g_m"], 1)
            g.memset(XP[:, :, :, 96:99], 1.0).then_inc(S["g_m"], 1)
            g.memset(CX[:, 0:1], -1.0).then_inc(S["g_m"], 1)
            dv = dst.rearrange("(b e) -> b e", e=EB)
            for c in range(50):
                g.wait_ge(S["v_q"], c // 10 + 1)
                if c >= 4:
                    g.wait_ge(S["a_blk"], c - 3)
                g.indirect_dma_start(BL[:, c % 4, :], None, dv,
                                     bass.IndirectOffsetOnAxis(ap=QI[:, c:c + 1], axis=0)).then_inc(d_bl[c % 4], 16)
            g.wait_ge(S["v_pc"], 1)
            g.wait_ge(S["d_i0"], 16)
            for c in range(NC):
                g.indirect_dma_start(RTD, bass.IndirectOffsetOnAxis(ap=SI[:, c:c + 1], axis=0), NV[:, c, :], None,
                                     bounds_check=NR - 1, oob_is_err=False).then_inc(S["d_sc0"], 16)
            g.wait_ge(S["v_rb"], 3)
            for b in range(2):
                g.wait_ge(d_ro[b], 16 * len(range(b, nq, 2)))
            g.wait_ge(S["d_i1"], 16 * NC)

            def rows(t):
                if t >= 3:
                    g.wait_ge(S["a_xp"], 4 * (t - 3) + 4)
                g.indirect_dma_start(REC[:, t % 3, :], None, RECD,
                                     bass.IndirectOffsetOnAxis(ap=E0[:, t:t + 1], axis=0)).then_inc(d_rec[t % 3], 16)

            def sums(t):
                g.wait_ge(S["a_dn"], t + 1)
                g.wait_ge(S["v_sev"], t + 1)
                g.indirect_dma_start(DTD, bass.IndirectOffsetOnAxis(ap=SX[:, t:t + 1], axis=0), DNS[:, t % 4, :], None,
                                     bounds_check=N - 1, oob_is_err=False).then_inc(d_st[t % 4], 16)

            rows(0)
            for t in range(NT):
                b = t % 3
                if t >= 2:
                    g.wait_ge(S["g_idx"], t - 1)
                    g.wait_ge(S["g_ev"], 4 * (t - 2) + 4)
                if t + 1 < NT:
                    rows(t + 1)
                g.wait_ge(d_rec[b], 16 * (t // 3 + 1))
                rec = REC[:, b, :].rearrange("p (j w) -> p j w", w=RW)
                if t >= 3:
                    g.wait_ge(d_h[b], 128 * (t // 3))
                g.tensor_tensor(IX[:, b, :].unsqueeze(2), rec[:, :, 40:41], INI[:, t, :].unsqueeze(2), ALU.add)\
                    .then_inc(S["g_idx"], 1)
                g.wait_ge(S["g_idx"], t + 1)
                if t >= 3:
                    g.wait_ge(S["v_mult"], 4 * (t - 3) + 4)
                for j in range(L):
                    g.indirect_dma_start(H[:, b, 16 * j:16 * j + 16], None, xt,
                                         bass.IndirectOffsetOnAxis(ap=IX[:, b, j:j + 1], axis=0)).then_inc(d_h[b], 16)
                n = 4 * t
                if t >= 2:
                    g.wait_ge(S["p_S"], t - 1)
                g.tensor_tensor(EV[:, :, :], rec[:, :, 0:16].bitcast(f32), VAL[:, t, :].unsqueeze(2).broadcast_to([128, L, 16]),
                                ALU.mult).then_inc(S["g_ev"], 1)
                g.wait_ge(S["g_ev"], n + 1)
                g.tensor_tensor(EA[:, :, :], EV[:, 0:4, :], EV[:, 4:8, :], ALU.add).then_inc(S["g_ev"], 1)
                g.wait_ge(S["g_ev"], n + 2)
                g.tensor_tensor(EB2[:, :, :], EA[:, 0:2, :], EA[:, 2:4, :], ALU.add).then_inc(S["g_ev"], 1)
                g.wait_ge(S["g_ev"], n + 3)
                g.tensor_tensor(ES[:, t % 2, :], EB2[:, 0, :], EB2[:, 1, :], ALU.add).then_inc(S["g_ev"], 1)
                if t >= 3:
                    sums(t - 3)
            for t in range(NT - 3, NT):
                sums(t)
            for b in range(4):
                g.wait_ge(d_st[b], 16 * len(range(b, NT, 4)))

        @block.scalar
        def _(a):
            a.wait_ge(S["d_w"], 16)
            a.activation(WH[:, 0, :], WF[:, :], ACT.Copy).then_inc(S["a_w"], 1)
            a.wait_ge(S["v_w"], 1)
            a.activation(WH[:, 1, :], WD[:, :], ACT.Copy).then_inc(S["a_w"], 1)

            def blk(c):
                a.wait_ge(d_bl[c % 4], 16 * (c // 4 + 1))
                if c >= 4:
                    a.wait_ge(S["v_blk"], c - 3)
                a.activation(BF[:, c % 4, :], BL[:, c % 4, :], ACT.Copy).then_inc(S["a_blk"], 1)

            a.wait_ge(S["d_sr"], 16)
            c = 0
            for q, (o, n) in enumerate(chunks):
                b = q % 2
                a.wait_ge(d_xi[b], 16 * (q // 2 + 1))
                if q >= 2:
                    a.wait_ge(d_ro[b], 16 * (q // 2))
                a.activation(RB[:, b, 0:n, 16:24].bitcast(bf16), XI[:, b, 0:n, :], ACT.Copy).then_inc(S["a_x0"], 1)
                a.activation(RB[:, b, 0:n, 0:16].bitcast(f32), XI[:, b, 0:n, :], ACT.Copy).then_inc(S["a_x0"], 1)
                a.copy(RB[:, b, 0:n, 40:41], SR[:, o:o + n].unsqueeze(2)).then_inc(S["a_x0"], 1)
                a.wait_ge(S["v_x1"], q + 1)
                a.activation(RB[:, b, 0:n, 24:32].bitcast(bf16), XD[:, 0:n, :], ACT.Copy).then_inc(S["a_x0"], 1)
                for _ in range(3):
                    if c < 50:
                        blk(c)
                        c += 1
            for c in range(c, 50):
                blk(c)

            def expand(t):
                a.wait_ge(d_rec[t % 3], 16 * (t // 3 + 1))
                if t >= 2:
                    a.wait_ge(S["p_T"], t - 1)
                rec = REC[:, t % 3, :].rearrange("p (j w) -> p j w", w=RW)
                x = XP[:, t % 2, :, :]
                a.activation(x[:, :, 0:48], rec[:, :, 16:40].bitcast(bf16), ACT.Copy).then_inc(S["a_xp"], 1)
                a.activation(x[:, :, 48:80], rec[:, :, 16:32].bitcast(bf16), ACT.Copy).then_inc(S["a_xp"], 1)
                a.activation(x[:, :, 80:96], rec[:, :, 16:24].bitcast(bf16), ACT.Copy).then_inc(S["a_xp"], 1)
                a.activation(x[:, :, 99:100], FLG[:, t, :].unsqueeze(2), ACT.Copy).then_inc(S["a_xp"], 1)

            def evac(t):
                a.wait_ge(S["p_T"], t + 1)
                if t >= 2:
                    a.wait_ge(S["p_W"], 4 * (t - 2) + 4)
                a.activation(LT[:, t % 2, :], PTB[0:K, :], ACT.Copy).then_inc(S["a_T"], 1)

            a.wait_ge(S["v_rb"], 3)
            a.wait_ge(S["g_m"], 8)
            expand(0)
            evac(0)
            expand(1)
            for t in range(NT + 1):
                if t + 1 < NT:
                    evac(t + 1)
                if t + 2 < NT:
                    expand(t + 2)
                if 1 <= t < NT:
                    a.wait_ge(S["v_del"], t)
                    a.activation(DR[:, :], DL[:, :], ACT.Relu, scale=-1.0).then_inc(S["a_rel"], 1)
                    a.wait_ge(S["a_rel"], t)
                    if t >= 2:
                        a.wait_ge(S["p_al"], t - 1)
                    a.activation(AL[:, :], DR[:, :], ACT.Exp, scale=-1.0).then_inc(S["a_al"], 1)
                if t < NT:
                    e = EM[:, t % 3, :].rearrange("p (x a o) -> p x a o", a=2, o=16)
                    a.wait_ge(S["v_sub"], t + 1)
                    for h in range(2):
                        v = e[:, 64 * h:64 * h + 64, 0, :]
                        a.activation(v, v, ACT.Exp).then_inc(S["a_exp"], 1)
                if t >= 1:
                    u = t - 1
                    a.wait_ge(S["p_sum"], u + 1)
                    if u >= 4:
                        a.wait_ge(d_st[u % 4], 16 * (u // 4))
                    a.activation(DNS[:, u % 4, 0:512], PDN[:, :], ACT.Copy).then_inc(S["a_dn"], 1)
            for c in range(NC):
                a.wait_ge(d_dt[c % 4], 16 * (c // 4 + 1))
                a.activation(SA[:, c, :], DTT[:, c % 4, 512:528], ACT.Copy).then_inc(S["a_sa"], 1)
            for k in range(2):
                a.wait_ge(S["v_var"], k + 1)
                a.activation(ST[:, 2, :], ST[:, 1, :], ACT.Sqrt).then_inc(S["a_z"], 1)

        @block.tensor
        def _(pe):
            pe.wait_ge(S["d_cs"], 16)
            pe.wait_ge(S["v_p"], 1)
            pe.matmul(PMB[:, 0:NB], ONE, FF[:, :], start=True, stop=True).then_inc(S["p_f"], 1)
            pe.wait_ge(S["v_p"], 3)
            pe.matmul(PMB[:, 0:1], TRI, INC[:, NC - 1:NC], start=True, stop=True).then_inc(S["p_o"], 1)
            pe.wait_ge(S["v_p"], 4)
            pe.transpose(PMB[0:4, 0:128], F4[:, :, RC - 1], IDN).then_inc(S["p_x"], 1)
            pe.wait_ge(S["v_p"], 5)
            pe.transpose(PMB[:, 0:4], CX[:, 0:128], CS[0:4, 0:4]).then_inc(S["p_y"], 1)
            pe.wait_ge(S["v_tr"], 6)
            for h in range(2):
                for k, a in enumerate((TN[:, :, 1:129], TE, TC, TS)):
                    b = (PMB, PDN)[h]
                    pe.transpose(b[:, 128 * k:128 * k + 120], a[:, h, :], CS[0:120, 0:120]).then_inc(S["p_t"], 1)
            pe.wait_ge(S["d_w2"], 160)
            pe.wait_ge(S["v_id"], 1)

            def T(t):
                pe.wait_ge(S["a_xp"], 4 * t + 4)
                if t >= 1:
                    pe.wait_ge(S["a_T"], t)
                for j in range(L):
                    i = pe.transpose(PTB[0:K, 128 * j:128 * j + 128], XP[:, t % 2, j, :], IDB[:, :])
                i.then_inc(S["p_T"], 1)

            def W(t, k):
                if k == 0:
                    pe.wait_ge(S["a_T"], t + 1)
                m = 4 * t + k
                if m >= 2:
                    pe.wait_ge(S["v_mult"], m - 1)
                for j in (2 * k, 2 * k + 1):
                    i = pe.matmul(PW[:, j % 4, :], LT[:, t % 2, 128 * j:128 * j + 128], WS[:, :], start=True, stop=True)
                i.then_inc(S["p_W"], 1)

            def gsum(t, *slots):
                for j in slots:
                    if j == 0:
                        pe.wait_ge(S["v_gm"], 2 * t + 1)
                        if t >= 1:
                            pe.wait_ge(S["a_dn"], t)
                    if j == 4:
                        pe.wait_ge(S["v_gm"], 2 * t + 2)
                    last = t == 0 and j == L - 1
                    i = pe.matmul(PDN[:, :], U[:, t % 3, :], EM[:, t % 3, 512 * j:512 * j + 512], start=(j == 0), stop=last)
                    if last:
                        i.then_inc(S["p_sum"], 1)

            def carry(t):
                if t >= 1:
                    pe.wait_ge(S["v_cm"], t)
                    pe.matmul(PDN[:, :], SEL[:, t % 3, :], DSC[:, :], start=False, stop=True).then_inc(S["p_sum"], 1)

            pe.wait_ge(S["v_tr"], 14)
            T(0)
            W(0, 0)
            W(0, 1)
            for t in range(NT + 1):
                if t >= 2:
                    gsum(t - 2, 3, 4)
                if t < NT:
                    W(t, 2)
                if t >= 2:
                    gsum(t - 2, 5)
                if t < NT:
                    W(t, 3)
                if t >= 2:
                    gsum(t - 2, 6, 7)
                    carry(t - 2)
                if t + 1 < NT:
                    T(t + 1)
                if t < NT:
                    pe.wait_ge(S["v_rmax"], t + 1)
                    pe.transpose(PMB[:, 0:128], MX[:, 0:128], IDN)
                    pe.transpose(PMB[:, 128:256], MX[:, 128:256], IDN).then_inc(S["p_mT"], 1)
                    pe.wait_ge(S["g_ev"], 4 * t + 4)
                    pe.wait_ge(S["v_u"], 2 * t + 2)
                    i = pe.matmul(PAL[:, 256:272], U[:, t % 3, :], ES[:, t % 2, :], start=True, stop=(t == 0))
                    if t >= 1:
                        pe.wait_ge(S["v_sev"], t)
                        i = pe.matmul(PAL[:, 256:272], SEL[:, t % 3, :], DNS[:, (t - 1) % 4, 512:528], start=False, stop=True)
                    i.then_inc(S["p_S"], 1)
                if t >= 1:
                    gsum(t - 1, 0)
                if t < NT:
                    pe.wait_ge(S["v_scan"], 4 * t + 4)
                    pe.transpose(PMB[:, 256:384], MT[:, t % 2, 0:128], IDN)
                    pe.transpose(PMB[:, 384:512], MT[:, t % 2, 128:256], IDN).then_inc(S["p_MB"], 1)
                if t >= 1:
                    gsum(t - 1, 1, 2)
                if 1 <= t < NT:
                    pe.wait_ge(S["a_al"], t)
                    pe.wait_ge(S["v_sev"], t + 1)
                    if t >= 2:
                        pe.wait_ge(S["v_cm"], t - 1)
                    for h in range(2):
                        i = pe.transpose(PAL[:, 128 * h:128 * h + 128], AL[:, h:h + 1].broadcast_to([128, 128]), IDN)
                    i.then_inc(S["p_al"], 1)
                if t + 1 < NT:
                    W(t + 1, 0)
                    W(t + 1, 1)
            gsum(NT - 1, 3, 4, 5, 6, 7)
            carry(NT - 1)

        @block.vector
        def _(v):
            chain = [0]
            lk = ctx.enter_context(nc.semaphore("v_link"))

            def link(i):
                chain[0] += 1
                i.then_inc(lk, 1)
                v.wait_ge(lk, chain[0])

            v.wait_ge(S["d_cs"], 16)
            v.tensor_copy(IDB[:, :], IDN).then_inc(S["v_id"], 1)
            v.wait_ge(S["d_f"], 16)
            v.tensor_copy(FF[:, :], FI[:, :]).then_inc(S["v_p"], 1)
            v.wait_ge(S["a_w"], 1)
            v.tensor_tensor(WD[:, :], WF[:, :], WH[:, 0, :], ALU.subtract).then_inc(S["v_w"], 1)
            v.wait_ge(S["a_w"], 2)
            v.tensor_tensor(WH[:, 2, :], WD[:, :], WH[:, 1, :], ALU.subtract).then_inc(S["v_w"], 1)

            def x_diff(q):
                o, n = chunks[q]
                b = q % 2
                v.wait_ge(S["a_x0"], 4 * q + 1)
                v.tensor_tensor(XD[:, 0:n, :], XI[:, b, 0:n, :], RB[:, b, 0:n, 16:24].bitcast(bf16), ALU.subtract).then_inc(S["v_x1"], 1)
                v.wait_ge(S["a_x0"], 4 * q + 4)
                v.tensor_tensor(RB[:, b, 0:n, 32:40].bitcast(bf16), XD[:, 0:n, :], RB[:, b, 0:n, 24:32].bitcast(bf16), ALU.subtract).then_inc(S["v_x3"], 1)
                v.wait_ge(S["v_x3"], q + 1)

            v.wait_ge(S["p_f"], 1)
            link(v.tensor_copy(FB[:, :], PMB[:, 0:NB]))
            for g5 in range(5):
                for c in range(10 * g5, 10 * g5 + 10):
                    link(v.tensor_scalar(JK[:, 0:NB], FB[:, :], NVAL[:, c:c + 1], None, ALU.is_lt, ALU.add,
                                         accum_out=BC[:, c:c + 1]))
                s = slice(10 * g5, 10 * g5 + 10)
                link(v.tensor_scalar(QF[:, s], BC[:, s], 1.0, 0.0, ALU.subtract, ALU.max))
                v.tensor_copy(QI[:, s], QF[:, s]).then_inc(S["v_q"], 1)
            c = 0

            def blk(c):
                v.wait_ge(S["a_blk"], c + 1)
                v.tensor_scalar(JK[:, :], BF[:, c % 4, :], NVAL[:, c:c + 1], None, ALU.is_lt, ALU.add,
                                accum_out=CB[:, c:c + 1]).then_inc(S["v_blk"], 1)
                v.wait_ge(S["v_blk"], c + 1)

            for q in range(nq):
                x_diff(q)
                for _ in range(3):
                    if c < 50:
                        blk(c)
                        c += 1
            for c in range(c, 50):
                blk(c)
            link(v.scalar_tensor_tensor(SS[:, :], QF[:, :], float(EB), CB[:, :], ALU.mult, ALU.add))
            link(v.tensor_tensor(DG[:, :], SS[:, 1:50], SS[:, 0:49], ALU.subtract))
            link(v.tensor_scalar(T1[:, :], DG[:, :], 7.0, None, ALU.add))
            link(v.tensor_copy(TI[:, :], T1[:, :]))
            link(v.tensor_scalar(TJ[:, :], TI[:, :], 3, None, ALU.logical_shift_right))
            link(v.tensor_copy(NRW[:, :], TJ[:, :]))
            v.wait_ge(S["g_m"], 8)
            i = v.tensor_tensor_scan(INC[:, :], NRW[:, :], ZR[:, 0:NC], 0.0, ALU.add, ALU.add)
            i.then_inc(S["v_p"], 2)
            v.wait_ge(S["v_p"], 3)
            link(v.tensor_tensor(T1[:, :], INC[:, :], NRW[:, :], ALU.subtract))
            v.wait_ge(S["p_o"], 1)
            link(v.tensor_copy(OFF[:, :], PMB[:, 0:1]))
            link(v.tensor_scalar(NV[:, :, 3], T1[:, :], OFF[:, 0:1], None, ALU.add))
            link(v.tensor_copy(NV[:, :, 0], NVAL[:, 0:NC]))
            link(v.tensor_copy(NV[:, :, 1], SS[:, 0:49]))
            link(v.tensor_copy(NV[:, :, 2], SS[:, 1:50]))
            link(v.tensor_scalar(T1[:, :], NRW[:, :], 0.0, NONE, ALU.is_equal, ALU.mult))
            v.tensor_tensor(SI[:, :], T1[:, :], NV[:, :, 3], ALU.add).then_inc(S["v_pc"], 1)
            v.wait_ge(S["d_rl"], 16)
            for f in range(4):
                i = v.tensor_tensor_scan(F4[:, f, :], RT[:, :, f], RT[:, :, f], -1.0, ALU.max, ALU.max)
                link(i)
            v.tensor_copy(CY[:, :], F4[:, :, RC - 1]).then_inc(S["v_p"], 1)
            v.wait_ge(S["p_x"], 1)
            link(v.tensor_copy(CT[:, :], PMB[0:4, 0:128]))
            v.tensor_tensor_scan(CX[:, 1:129], CT[:, :], CT[:, :], -1.0, ALU.max, ALU.max).then_inc(S["v_p"], 1)
            v.wait_ge(S["p_y"], 1)
            link(v.tensor_copy(CY[:, :], PMB[:, 0:4]))
            link(v.tensor_tensor(F5[:, :, :], F4[:, :, :], CY[:, :].unsqueeze(2).broadcast_to([128, 4, RC]), ALU.max))
            link(v.tensor_tensor(R1[:, :], RID, F5[:, 3, :], ALU.subtract))
            link(v.scalar_tensor_tensor(R2[:, :], R1[:, :], float(L), F5[:, 1, :], ALU.mult, ALU.add))
            link(v.tensor_tensor(R3[:, :], R2[:, :], F5[:, 2, :], ALU.is_ge))
            link(v.tensor_tensor(R1[:, :], F5[:, 2, :], R2[:, :], ALU.subtract))
            v.tensor_scalar(RCN[:, :], R1[:, :], float(L), 0.0, ALU.min, ALU.max).then_inc(S["v_rr"], 1)
            v.wait_ge(S["v_rr"], 1)
            link(v.scalar_tensor_tensor(R1[:, :], R3[:, :], -1.0, R2[:, :], ALU.mult, ALU.mult))
            v.tensor_tensor(RE[:, :], R2[:, :], R1[:, :], ALU.add).then_inc(S["v_rr"], 1)
            v.scalar_tensor_tensor(RN[:, :], R3[:, :], float(N), F5[:, 0, :], ALU.mult, ALU.max).then_inc(S["v_rr"], 1)
            v.wait_ge(S["d_tl"], 64)
            mk = MKT[:, :, :].rearrange("t h (k r) -> t h k r", k=3)
            v.tensor_copy(mk[:, :, 0, :], TN[:, :, 1:129]).then_inc(S["v_tr"], 1)
            v.tensor_tensor(mk[:, :, 1, :], TN[:, :, 1:129], TN[:, :, 0:128], ALU.not_equal).then_inc(S["v_tr"], 1)
            v.tensor_tensor(mk[:, :, 2, :], TN[:, :, 1:129], TN[:, :, 2:130], ALU.not_equal).then_inc(S["v_tr"], 1)
            v.wait_ge(S["v_tr"], 3)
            link(v.tensor_scalar(TS[:, :, :], mk[:, :, 2, :], -NONE, NONE, ALU.mult, ALU.add))
            v.wait_ge(S["v_tr"], 3)
            v.tensor_scalar(mk[:, :, 1, :], mk[:, :, 1, :], BIG, None, ALU.mult).then_inc(S["v_tr"], 1)
            v.tensor_scalar(mk[:, :, 2, :], mk[:, :, 2, :], BIG, None, ALU.mult).then_inc(S["v_tr"], 1)
            v.tensor_tensor(TS[:, :, :], TS[:, :, :], TN[:, :, 1:129], ALU.add).then_inc(S["v_tr"], 1)
            for h in range(2):
                v.wait_ge(S["p_t"], 4 * h + 4)
                b = (PMB, PDN)[h]
                for k, a in enumerate((NID, E0, CNT, SX)):
                    v.tensor_copy(a[:, 120 * h:120 * h + 120], b[:, 128 * k:128 * k + 120]).then_inc(S["v_tr"], 1)
            v.wait_ge(S["v_tr"], 14)
            link(v.tensor_tensor(INV[:, :, :], IO8.unsqueeze(1).broadcast_to([128, RC, L]),
                                 CNT[:, :].unsqueeze(2).broadcast_to([128, RC, L]), ALU.is_ge))
            v.tensor_scalar(VAL[:, :, :], INV[:, :, :], -1.0, 1.0, ALU.mult, ALU.add).then_inc(S["v_rb"], 1)
            v.tensor_scalar(INI[:, :, :], INV[:, :, :], float(N), None, ALU.mult).then_inc(S["v_rb"], 1)
            v.tensor_copy(FLG[:, :, :], INV[:, :, :]).then_inc(S["v_rb"], 1)

            for t in range(NT + 1):
                b, e = t % 3, t % 2
                if t < NT:
                    v.wait_ge(d_mk[b], 16 * (t // 3 + 1))
                    if t >= 3:
                        v.wait_ge(S["p_sum"], t - 2)
                    v.tensor_scalar(U[:, b, :], MK[:, b, 0:128], NID[:, t:t + 1], None, ALU.is_equal).then_inc(S["v_u"], 1)
                    v.tensor_scalar(SEL[:, b, :], MK[:, b, 0:128], NID[:, max(t - 1, 0):max(t - 1, 0) + 1], E127,
                                    ALU.is_equal, ALU.mult).then_inc(S["v_u"], 1)
                    v.wait_ge(d_h[b], 128 * (t // 3 + 1))
                    for k in range(4):
                        v.wait_ge(S["p_W"], 4 * t + k + 1)
                        w = PW[:, 2 * (k % 2):2 * (k % 2) + 2, :].rearrange("p j (i c) -> p (j i) c", c=32)
                        hb = H[:, b, 32 * k:32 * k + 32].unsqueeze(2).broadcast_to([128, 32, 32])
                        v.tensor_tensor(EM[:, b, 1024 * k:1024 * k + 1024].rearrange("p (x c) -> p x c", c=32), w, hb,
                                        ALU.mult).then_inc(S["v_mult"], 1)
                    v.wait_ge(S["v_mult"], 4 * t + 4)
                    if t >= 1:
                        v.wait_ge(S["p_mT"], t)
                    em = EM[:, b, :].rearrange("p (j i a o) -> p i a o j", j=L, a=2, o=16)
                    v.tensor_reduce(MX[:, :].rearrange("p (i o) -> p i o", o=16), em[:, :, 0, :, :], AX.X, ALU.max)\
                        .then_inc(S["v_rmax"], 1)

                def gm(u, h):
                    v.wait_ge(S["a_exp"], 2 * u + h + 1)
                    x = EM[:, u % 3, 2048 * h:2048 * h + 2048].rearrange("p (x a o) -> p x a o", a=2, o=16)
                    v.tensor_tensor(x[:, :, 1, :], x[:, :, 1, :], x[:, :, 0, :], ALU.mult).then_inc(S["v_gm"], 1)

                if t >= 1:
                    gm(t - 1, 0)
                if t < NT:
                    v.wait_ge(S["p_mT"], t + 1)
                    for h in range(2):
                        s = slice(128 * h, 128 * h + 128)
                        init = BIG if t == 0 else MT[:, 1 - e, 128 * h + 127:128 * h + 128]
                        v.tensor_tensor_scan(MF[:, s], MK[:, b, 128:256], PMB[:, s], init, ALU.add, ALU.max)\
                            .then_inc(S["v_scan"], 1)
                    for h in range(2):
                        s = slice(128 * h, 128 * h + 128)
                        v.wait_ge(S["v_scan"], 4 * t + h + 1)
                        v.tensor_tensor_scan(MT[:, e, s][:, ::-1], MK[:, b, 256:384][:, ::-1], MF[:, s][:, ::-1], BIG,
                                             ALU.add, ALU.max).then_inc(S["v_scan"], 1)
                    v.wait_ge(S["v_scan"], 4 * t + 4)
                    if t >= 1:
                        if t >= 2:
                            v.wait_ge(S["a_rel"], t - 1)
                        m0 = MT[:, 1 - e, :].rearrange("p (h r) -> p h r", r=128)[:, :, 127]
                        m1 = MT[:, e, :].rearrange("p (h r) -> p h r", r=128)[:, :, 0]
                        v.tensor_tensor(DL[:, :], m0, m1, ALU.subtract).then_inc(S["v_del"], 1)
                    v.wait_ge(S["p_S"], t + 1)
                    if t >= 4:
                        v.wait_ge(d_st[t % 4], 16 * (t // 4))
                    v.tensor_copy(DNS[:, t % 4, 512:528], PAL[:, 256:272]).then_inc(S["v_sev"], 1)
                if t >= 1:
                    gm(t - 1, 1)
                if t >= 2:
                    u = t - 1
                    v.wait_ge(S["a_dn"], u)
                    v.wait_ge(S["p_al"], u)
                    if u >= 2:
                        v.wait_ge(S["p_sum"], u)
                    dn = DNS[:, (u - 1) % 4, 0:512].rearrange("p (i a o) -> p i a o", a=2, o=16)
                    al = PAL[:, 0:256].rearrange("p (i o) -> p i o", o=16).unsqueeze(2).broadcast_to([128, 16, 2, 16])
                    v.tensor_tensor(DSC[:, :].rearrange("p (i a o) -> p i a o", a=2, o=16), dn, al, ALU.mult)\
                        .then_inc(S["v_cm"], 1)
                if t < NT:
                    v.wait_ge(S["p_MB"], t + 1)
                    x = EM[:, b, :].rearrange("p (j i a o) -> p j i a o", j=L, a=2, o=16)
                    mb = PMB[:, 256:512].rearrange("p (i o) -> p i o", o=16)
                    v.tensor_tensor(x[:, :, :, 0, :], x[:, :, :, 0, :], mb.unsqueeze(1).broadcast_to([128, L, 16, 16]),
                                    ALU.subtract).then_inc(S["v_sub"], 1)
            for c in range(NC):
                v.wait_ge(d_dt[c % 4], 16 * (c // 4 + 1))
                d = DTT[:, c % 4, 0:512].rearrange("p (i a o) -> p i a o", a=2, o=16)
                v.reciprocal(RCP[:, :].rearrange("p (i o) -> p i o", o=16), d[:, :, 0, :]).then_inc(S["v_e"], 1)
                v.wait_ge(S["v_e"], 3 * c + 1)
                v.tensor_tensor(PRD[:, :].rearrange("p (i o) -> p i o", o=16), d[:, :, 1, :],
                                RCP[:, :].rearrange("p (i o) -> p i o", o=16), ALU.mult).then_inc(S["v_e"], 1)
                v.wait_ge(S["v_e"], 3 * c + 2)
                v.tensor_reduce(FT[:, c, :], PRD[:, :].rearrange("p (i o) -> p o i", o=16), AX.X, ALU.add)\
                    .then_inc(S["v_e"], 1)
            v.wait_ge(S["v_e"], 3 * NC)
            v.wait_ge(S["a_sa"], NC)
            v.wait_ge(S["d_xn"], 16)

            def bc(a):
                return a.unsqueeze(2).broadcast_to([128, NC, 16])

            def layernorm(k):
                link(v.tensor_reduce(ST[:, 0, :], Y[:, :, :], AX.X, ALU.add))
                link(v.tensor_scalar(ST[:, 3, :], ST[:, 0, :], 1.0 / 16, None, ALU.mult))
                link(v.tensor_tensor(XN[:, :, :], Y[:, :, :], bc(ST[:, 3, :]), ALU.subtract))
                link(v.tensor_tensor(Y2[:, :, :], XN[:, :, :], XN[:, :, :], ALU.mult))
                link(v.tensor_reduce(ST[:, 0, :], Y2[:, :, :], AX.X, ALU.add))
                v.tensor_scalar(ST[:, 1, :], ST[:, 0, :], 1.0 / 16, 1.0e-5, ALU.mult, ALU.add).then_inc(S["v_var"], 1)
                v.wait_ge(S["a_z"], k + 1)
                link(v.reciprocal(ST[:, 0, :], ST[:, 2, :]))
                return v.tensor_tensor(Y2[:, :, :], XN[:, :, :], bc(ST[:, 0, :]), ALU.mult)

            link(v.tensor_tensor(Y[:, :, :], XN[:, :, :], FT[:, :, :], ALU.add))
            link(layernorm(0))
            link(v.tensor_scalar(T1[:, :], DG[:, :], 1.0, None, ALU.max))
            link(v.reciprocal(RCN2[:, :], T1[:, :]))
            link(v.tensor_tensor(SA[:, :, :], SA[:, :, :], bc(RCN2[:, :]), ALU.mult))
            link(v.tensor_tensor(Y[:, :, :], SA[:, :, :], Y2[:, :, :], ALU.add))
            layernorm(1).then_inc(S["v_fin"], 1)


def kernel(**inputs):
    import numpy as np
    import concourse.bacc as bacc
    from concourse.bass_utils import run_bass_kernel_spmd as run

    x, ea = np.asarray(inputs["x"]), np.asarray(inputs["edge_attr_16"])
    src, dst = np.asarray(inputs["src"]), np.asarray(inputs["dst"])
    xt = np.concatenate([x, np.ones((N, 16), x.dtype)])
    eap = np.concatenate([ea, np.zeros((EP - E, 16), ea.dtype)])
    srcp = np.concatenate([src, np.zeros(EP - E, src.dtype)])
    dstp = np.concatenate([dst, np.full(NB * EB - E, 1 << 20, dst.dtype)])
    wa, wm = (np.asarray(inputs[f"L0_gnn_W_{k}"]).reshape(16, 16, 1, 16) for k in ("attn", "msg"))
    ba, bm = (np.asarray(inputs[f"L0_gnn_b_{k}"]).reshape(1, 16, 1, 16) for k in ("attn", "msg"))
    wc = np.concatenate([np.concatenate([wa, wm], 2), np.concatenate([ba, bm], 2)], 0).reshape(17, 512)
    cst = np.zeros((128, 692), np.float32)
    p = np.arange(128)
    cst[:, 0:128] = np.eye(128)
    cst[:, 128:256] = p[:, None] < p[None, :]
    cst[127, 256] = 1
    cst[:, 257:307] = p[:, None] * NC + np.arange(50)
    cst[:, 307:547] = p[:, None] * RC + np.arange(RC)
    cst[:, 547:555] = np.arange(8)
    cst[0, 555:557] = -1, -2
    cst[0, 557:685] = 1

    nc = bacc.Bacc("TRN2", target_bir_lowering=False, num_devices=1)
    arrays, args = {}, []
    for name, a in (("xt", xt), ("dst", dstp), ("src", srcp), ("ea", eap), ("wc", wc), ("cst", cst)):
        a = np.ascontiguousarray(a)
        arrays[f"in_{name}"] = a
        args.append(nc.dram_tensor(f"in_{name}", a.shape, mybir.dt.from_np(a.dtype), kind="ExternalInput").ap())
    o = nc.dram_tensor("out_0", (N, 16), mybir.dt.float32, kind="ExternalOutput").ap()
    gnn_kernel(nc, *args, o)
    r = run(nc, [arrays], core_ids=[0])
    return r.results[0]["out_0"]
```

```python
import concourse.bass as bass
from concourse import mybir
from contextlib import ExitStack

N = 6250
E = 200000
L = 8
NC = 49
NP = 128 * NC
EB = 512
NB = 391
EC = 1563
EP = 128 * EC
NT = 239
RC = 240
NR = 128 * RC
RW = 41
DW = 528
K = 100
BIG = -1.0e35
NONE = 100000.0
PADS = -1.0e25


def gnn_kernel(nc, xt, dst, src, ea, wc, cst, out):
    f32, bf16, i32 = mybir.dt.float32, mybir.dt.bfloat16, mybir.dt.int32
    ALU, ACT, AX = mybir.AluOpType, mybir.ActivationFunctionType, mybir.AxisListType
    RECD = nc.dram_tensor("rec_d", [EP, RW], i32, kind="Internal").ap()
    RTD = nc.dram_tensor("rt_d", [NR, 4], f32, kind="Internal").ap()
    NIDD = nc.dram_tensor("nid_d", [NR + 2], f32, kind="Internal").ap()
    E0D = nc.dram_tensor("e0_d", [NR], f32, kind="Internal").ap()
    CND = nc.dram_tensor("cn_d", [NR], f32, kind="Internal").ap()
    MKD = nc.dram_tensor("mk_d", [RC, 384], f32, kind="Internal").ap()
    DTD = nc.dram_tensor("dt_d", [NP, DW], f32, kind="Internal").ap()

    ctx = ExitStack()
    with ctx:
        def sb(name, shape, dt=f32):
            return ctx.enter_context(nc.sbuf_tensor(name, shape, dt))

        def sem(name):
            return ctx.enter_context(nc.semaphore(name))

        CS = sb("CS", [128, 692])
        IDN, TRI, E127 = CS[:, 0:128], CS[:, 128:256], CS[:, 256:257]
        NVAL, RID, IO8 = CS[:, 257:307], CS[:, 307:547], CS[:, 547:555]
        SENT, ONE = CS[0:1, 555:557], CS[0:1, 557:685]
        IDB = sb("IDB", [128, 128], bf16)
        FI = sb("FI", [1, NB], i32)
        FF = sb("FF", [1, NB])
        FB = sb("FB", [128, NB])
        JK = sb("JK", [128, 512])
        BC = sb("BC", [128, 50])
        QF = sb("QF", [128, 50])
        QI = sb("QI", [128, 50], i32)
        EM = sb("EM", [128, 3, L * 512])
        BF = EM[:, 1, :].rearrange("p (b e) -> p b e", b=8)
        CB = sb("CB", [128, 50])
        SS = sb("SS", [128, 50])
        DG = sb("DG", [128, NC])
        T1 = sb("T1", [128, NC])
        TI = sb("TI", [128, NC], i32)
        TJ = sb("TJ", [128, NC], i32)
        NRW = sb("NRW", [128, NC])
        INC = sb("INC", [128, NC])
        OFF = sb("OFF", [128, 1])
        NV = sb("NV", [128, NC, 4])
        SI = sb("SI", [128, NC], i32)
        ZR = sb("ZR", [128, RC])
        M1 = EM[:, 2, 0:960]
        RT = EM[:, 2, 960:1920].rearrange("p (c w) -> p c w", w=4)
        F4 = EM[:, 2, 1920:2880].rearrange("p (w c) -> p w c", w=4)
        F5 = EM[:, 2, 2880:3840].rearrange("p (w c) -> p w c", w=4)
        CX = sb("CX", [4, 132])
        CT = sb("CT", [4, 128])
        CY = sb("CY", [128, 4])
        R1 = sb("R1", [128, RC])
        R2 = sb("R2", [128, RC])
        R3 = sb("R3", [128, RC])
        RE = sb("RE", [128, RC])
        RCN = sb("RCN", [128, RC])
        RN = sb("RN", [128, RC])
        TN = sb("TN", [120, 2, 130])
        TE = sb("TE", [120, 2, 128])
        TC = sb("TC", [120, 2, 128])
        TS = sb("TS", [120, 2, 128])
        MKT = sb("MKT", [120, 2, 384])
        NID = sb("NID", [128, RC])
        E0 = sb("E0", [128, RC], i32)
        CNT = sb("CNT", [128, RC])
        SX = sb("SX", [128, RC], i32)
        INV = EM[:, 0, 2176:4096].rearrange("p (c j) -> p c j", j=L)
        VAL = sb("VAL", [128, RC, L])
        INI = sb("INI", [128, RC, L], i32)
        FLG = sb("FLG", [128, RC, L], bf16)
        DI = sb("DI", [128, DW])
        WF = sb("WF", [17, 512])
        WH = sb("WH", [17, 3, 512], bf16)
        WD = sb("WD", [17, 512])
        FLW = sb("FLW", [1, 512], bf16)
        WS = sb("WS", [K, 512], bf16)
        CH = 48
        chunks = [(o, min(CH, EC - o)) for o in range(0, EC, CH)]
        XI = EM[:, 0, 0:3 * CH * 16].rearrange("p (b c k) -> p b c k", b=3, k=16)
        SR = sb("SR", [128, EC], i32)
        XD = EM[:, 0, 3 * CH * 16:5 * CH * 16].rearrange("p (b c k) -> p b c k", b=2, k=16)
        RB = sb("RB", [128, 3, CH, RW], i32)
        REC = sb("REC", [128, 3, L * RW], i32)
        IX = sb("IX", [128, 3, L], i32)
        H = sb("H", [128, 3, L * 16])
        XP = sb("XP", [128, 2, L, K], bf16)
        LT = sb("LT", [K, 2, L * 128], bf16)
        MX = sb("MX", [128, 256])
        MF = sb("MF", [128, 256])
        MT = sb("MT", [128, 2, 256])
        MK = sb("MK", [128, 3, 384])
        U = sb("U", [128, 3, 128])
        CM = sb("CM", [128, 3, 128])
        UA = sb("UA", [128, 2, 128])
        DR = sb("DR", [128, 2])
        AL = sb("AL", [128, 2, 2])
        CC = sb("CC", [128, 4])
        DGM = sb("DGM", [128, 4, 128])
        SE = sb("SE", [128, 2, 16])
        DNS = sb("DNS", [128, 4, DW])
        EV = sb("EV", [128, 2, L, 16])
        EH = sb("EH", [128, 4, 16])
        EQ = sb("EQ", [128, 2, 2, 16])
        GC = 7
        NG = NC // GC
        DTT = EM[:, 0:2, 0:GC * DW].rearrange("p b (c w) -> p b c w", w=DW)
        LN = EM[:, 2, 0:256 * GC]
        RR = EM[:, 2, 256 * GC:512 * GC]
        TP = sb("TP", [128, 256 * GC])
        FT = sb("FT", [128, NC, 16])
        SA = sb("SA", [128, NC, 16])
        XN = sb("XN", [128, NC, 16])
        Y = sb("Y", [128, NC, 16])
        Y2 = sb("Y2", [128, NC, 16])
        ST = sb("ST", [128, 4, NC])
        RCN2 = sb("RCN2", [128, NC])

        PW = ctx.enter_context(nc.psum_tensor("PW", [128, 4, 512], f32))
        PTB = ctx.enter_context(nc.psum_tensor("PTB", [128, L * 128], bf16))
        PMB = ctx.enter_context(nc.psum_tensor("PMB", [128, 512], f32))
        PDN = ctx.enter_context(nc.psum_tensor("PDN", [128, 512], f32))
        PAL = ctx.enter_context(nc.psum_tensor("PAL", [128, 512], f32))

        names = """d_cs d_f d_w d_w2 d_sr d_i0 d_i1 d_sc0 d_rl d_s1 d_tl d_mkd d_out d_xn
            v_id v_p v_pc v_q v_blk v_rr v_tr v_rb v_w v_x1 v_x3 v_nr
            v_mult v_rmax v_scan v_gm v_sub v_e v_var v_fin
            p_f p_o p_x p_y p_t p_T p_W p_mT p_S p_MB p_X p_sum
            a_w a_hi a_mid a_fs a_xp a_T a_exp a_rel a_al a_dn a_z a_sa a_u a_c a_se a_r a_sev
            g_m g_idx g_ev""".split()
        S = {n: sem(n) for n in names}
        d_xi = [sem(f"d_xi{i}") for i in range(3)]
        d_ro = [sem(f"d_ro{i}") for i in range(3)]
        d_bl = [sem(f"d_bl{i}") for i in range(8)]
        d_rec = [sem(f"d_rec{i}") for i in range(3)]
        d_h = [sem(f"d_h{i}") for i in range(3)]
        d_mk = [sem(f"d_mk{i}") for i in range(3)]
        d_st = [sem(f"d_st{i}") for i in range(4)]
        d_dt = [sem(f"d_dt{i}") for i in range(2)]
        nq = len(chunks)

        block = ctx.enter_context(nc.Block())

        @block.sync
        def _(sp):
            sp.dma_start(CS[:, :], cst).then_inc(S["d_cs"], 16)
            sp.dma_start(FI[:, :], dst.rearrange("(b e) -> e b", e=EB)[0:1, :],
                         allow_slow_non_contiguous=True).then_inc(S["d_f"], 16)
            sp.dma_start(WF[:, :], wc).then_inc(S["d_w"], 16)
            sp.dma_start(SR[:, :], src.rearrange("(p c) -> p c", c=EC)).then_inc(S["d_sr"], 16)
            eav = ea.rearrange("(p c) k -> p c k", c=EC)
            recv = RECD.rearrange("(p c) w -> p c w", c=EC)

            def load(q):
                o, n = chunks[q]
                if q >= 3:
                    sp.wait_ge(S["a_hi"], q - 2)
                    sp.wait_ge(S["a_fs"], 2 * (q - 3) + 2)
                    sp.wait_ge(S["v_x1"], q - 2)
                sp.dma_start(XI[:, q % 3, 0:n, :], eav[:, o:o + n, :]).then_inc(d_xi[q % 3], 16)

            for q in range(3):
                load(q)
            sp.wait_ge(S["a_w"], 2)
            sp.wait_ge(S["v_w"], 2)
            sp.wait_ge(S["g_m"], 8)
            for k, part in enumerate((0, 0, 0, 1, 1, 2)):
                sp.dma_start(WS[16 * k:16 * k + 16, :], WH[0:16, part, :]).then_inc(S["d_w2"], 16)
            for k in range(3):
                sp.dma_start(WS[96 + k:97 + k, :], WH[16:17, k, :]).then_inc(S["d_w2"], 16)
            sp.dma_start(WS[99:100, :], FLW[:, :]).then_inc(S["d_w2"], 16)
            sp.dma_start(RTD.rearrange("(p c) w -> p (c w)", c=RC), M1[:, :]).then_inc(S["d_i0"], 16)
            for q, (o, n) in enumerate(chunks):
                sp.wait_ge(S["a_mid"], q + 1)
                sp.wait_ge(S["a_fs"], 2 * q + 2)
                sp.wait_ge(S["v_x3"], q + 1)
                sp.dma_start(recv[:, o:o + n, :], RB[:, q % 3, 0:n, :]).then_inc(d_ro[q % 3], 16)
                if q + 3 < nq:
                    load(q + 3)
            sp.dma_start(DTD.rearrange("(c p) w -> p c w", p=128), DI[:, :].unsqueeze(1).broadcast_to([128, NC, DW]))\
              .then_inc(S["d_i1"], 16)
            sp.wait_ge(S["d_sc0"], 16 * NC)
            sp.dma_start(RT[:, :, :], RTD.rearrange("(p c) w -> p c w", c=RC)).then_inc(S["d_rl"], 16)
            sp.wait_ge(S["v_rr"], 3)
            sp.dma_start(E0D.rearrange("(p c) -> p c", c=RC), RE[:, :]).then_inc(S["d_s1"], 16)
            sp.dma_start(CND.rearrange("(p c) -> p c", c=RC), RCN[:, :]).then_inc(S["d_s1"], 16)
            sp.dma_start(NIDD[1:NR + 1].rearrange("(p c) -> p c", c=RC), RN[:, :]).then_inc(S["d_s1"], 16)
            sp.dma_start(NIDD[0:1].unsqueeze(0), SENT[:, 0:1]).then_inc(S["d_s1"], 16)
            sp.dma_start(NIDD[NR + 1:NR + 2].unsqueeze(0), SENT[:, 1:2]).then_inc(S["d_s1"], 16)
            sp.wait_ge(S["d_s1"], 80)
            v0 = NIDD[0:NR].rearrange("(h t r) -> t h r", h=2, r=128)
            v1 = NIDD[2:NR + 2].rearrange("(h t r) -> t h r", h=2, r=128)
            sp.dma_start(TN[:, :, 0:128], v0).then_inc(S["d_tl"], 16)
            sp.dma_start(TN[:, :, 128:130], v1[:, :, 126:128]).then_inc(S["d_tl"], 16)
            sp.dma_start(TE[:, :, :], E0D.rearrange("(h t r) -> t h r", h=2, r=128)).then_inc(S["d_tl"], 16)
            sp.dma_start(TC[:, :, :], CND.rearrange("(h t r) -> t h r", h=2, r=128)).then_inc(S["d_tl"], 16)
            sp.wait_ge(S["v_tr"], 6)
            sp.dma_start(MKD.rearrange("(h t) r -> t h r", h=2), MKT[:, :, :]).then_inc(S["d_mkd"], 16)
            sp.wait_ge(S["d_mkd"], 16)
            sp.dma_start(XN[:, :, :], xt[0:NP, :].rearrange("(p c) k -> p c k", c=NC)).then_inc(S["d_xn"], 16)
            for t in range(NT):
                if t >= 3:
                    sp.wait_ge(S["v_scan"], 4 * (t - 3) + 4)
                    sp.wait_ge(S["a_u"], 4 * (t - 2) + 2)
                sp.dma_start(MK[:, t % 3, :], MKD[t:t + 1, :].broadcast_to([128, 384])).then_inc(d_mk[t % 3], 16)
            for b in range(4):
                sp.wait_ge(d_st[b], 16 * len(range(b, NT, 4)))
            dtv = DTD.rearrange("(p c) w -> p c w", c=NC)
            for g in range(NG):
                if g >= 2:
                    sp.wait_ge(S["v_e"], 4 * (g - 2) + 3)
                    sp.wait_ge(S["a_sa"], g - 1)
                sp.dma_start(DTT[:, g % 2, :, :], dtv[:, GC * g:GC * g + GC, :]).then_inc(d_dt[g % 2], 16)
            sp.wait_ge(S["v_fin"], 1)
            sp.dma_start(out[0:127 * NC, :].rearrange("(p c) k -> p c k", c=NC), Y2[0:127, :, :]).then_inc(S["d_out"], 16)
            sp.dma_start(out[127 * NC:N, :].unsqueeze(0), Y2[127:128, 0:N - 127 * NC, :]).then_inc(S["d_out"], 16)
            sp.wait_ge(S["d_out"], 32)

        @block.gpsimd
        def _(g):
            g.memset(FLW[:, :], 0.0).then_inc(S["g_m"], 1)
            g.wait_ge(S["g_m"], 1)
            flv = FLW[:, :].rearrange("p (i a o) -> p i a o", a=2, o=16)
            g.memset(M1[:, :], -1.0).then_inc(S["g_m"], 1)
            g.memset(DI[:, :], 0.0).then_inc(S["g_m"], 1)
            g.wait_ge(S["g_m"], 3)
            g.memset(DI[:, 0:256], 1.0).then_inc(S["g_m"], 1)
            g.memset(flv[:, :, 0, :], PADS).then_inc(S["g_m"], 1)
            g.memset(ZR[:, :], 0.0).then_inc(S["g_m"], 1)
            g.memset(XP[:, :, :, 96:99], 1.0).then_inc(S["g_m"], 1)
            g.memset(CX[:, 0:1], -1.0).then_inc(S["g_m"], 1)
            dv = dst.rearrange("(b e) -> b e", e=EB)
            for c in range(50):
                g.wait_ge(S["v_q"], c // 10 + 1)
                if c >= 8:
                    g.wait_ge(S["v_blk"], c - 7)
                g.indirect_dma_start(BF[:, c % 8, :], None, dv,
                                     bass.IndirectOffsetOnAxis(ap=QI[:, c:c + 1], axis=0)).then_inc(d_bl[c % 8], 16)
            g.wait_ge(S["v_pc"], 1)
            g.wait_ge(S["d_i0"], 16)
            for c in range(NC):
                g.indirect_dma_start(RTD, bass.IndirectOffsetOnAxis(ap=SI[:, c:c + 1], axis=0), NV[:, c, :], None,
                                     bounds_check=NR - 1, oob_is_err=False).then_inc(S["d_sc0"], 16)
            g.wait_ge(S["v_rb"], 3)
            for b in range(3):
                g.wait_ge(d_ro[b], 16 * len(range(b, nq, 3)))

            def rows(t):
                if t >= 3:
                    g.wait_ge(S["a_xp"], 4 * (t - 3) + 4)
                g.indirect_dma_start(REC[:, t % 3, :], None, RECD,
                                     bass.IndirectOffsetOnAxis(ap=E0[:, t:t + 1], axis=0)).then_inc(d_rec[t % 3], 16)

            def sums(t):
                if t == 0:
                    g.wait_ge(S["d_i1"], 16)
                g.wait_ge(S["a_dn"], t + 1)
                g.wait_ge(S["a_sev"], t + 1)
                g.indirect_dma_start(DTD, bass.IndirectOffsetOnAxis(ap=SX[:, t:t + 1], axis=0), DNS[:, t % 4, :], None,
                                     bounds_check=N - 1, oob_is_err=False).then_inc(d_st[t % 4], 16)

            rows(0)
            for t in range(NT):
                b = t % 3
                if t >= 2:
                    g.wait_ge(S["g_idx"], t - 1)
                    g.wait_ge(S["g_ev"], 3 * (t - 1))
                if t + 1 < NT:
                    rows(t + 1)
                g.wait_ge(d_rec[b], 16 * (t // 3 + 1))
                rec = REC[:, b, :].rearrange("p (j w) -> p j w", w=RW)
                if t >= 3:
                    g.wait_ge(d_h[b], 128 * (t // 3))
                g.tensor_tensor(IX[:, b, :].unsqueeze(2), rec[:, :, 40:41], INI[:, t, :].unsqueeze(2), ALU.add)\
                    .then_inc(S["g_idx"], 1)
                g.wait_ge(S["g_idx"], t + 1)
                if t >= 3:
                    g.wait_ge(S["v_mult"], 4 * (t - 3) + 4)
                for j in range(L):
                    g.indirect_dma_start(H[:, b, 16 * j:16 * j + 16], None, xt,
                                         bass.IndirectOffsetOnAxis(ap=IX[:, b, j:j + 1], axis=0)).then_inc(d_h[b], 16)
                if t >= 2:
                    g.wait_ge(S["p_S"], t - 1)
                g.tensor_tensor(EV[:, t % 2, :, :], rec[:, :, 0:16].bitcast(f32),
                                VAL[:, t, :].unsqueeze(2).broadcast_to([128, L, 16]), ALU.mult).then_inc(S["g_ev"], 1)
                g.wait_ge(S["g_ev"], 3 * t + 1)
                g.tensor_tensor(EH[:, :, :], EV[:, t % 2, 0:4, :], EV[:, t % 2, 4:8, :], ALU.add).then_inc(S["g_ev"], 1)
                g.wait_ge(S["g_ev"], 3 * t + 2)
                g.tensor_tensor(EQ[:, t % 2, :, :], EH[:, 0:2, :], EH[:, 2:4, :], ALU.add).then_inc(S["g_ev"], 1)
                if t >= 3:
                    sums(t - 3)
            for t in range(NT - 3, NT):
                sums(t)
            for b in range(4):
                g.wait_ge(d_st[b], 16 * len(range(b, NT, 4)))

        @block.scalar
        def _(a):
            a.wait_ge(S["d_w"], 16)
            a.activation(WH[:, 0, :], WF[:, :], ACT.Copy).then_inc(S["a_w"], 1)
            a.wait_ge(S["v_w"], 1)
            a.activation(WH[:, 1, :], WD[:, :], ACT.Copy).then_inc(S["a_w"], 1)

            a.wait_ge(S["d_sr"], 16)

            def mid(q):
                n = chunks[q][1]
                a.wait_ge(S["v_x1"], q + 1)
                a.activation(RB[:, q % 3, 0:n, 24:32].bitcast(bf16), XD[:, q % 2, 0:n, :], ACT.Copy).then_inc(S["a_mid"], 1)

            for q, (o, n) in enumerate(chunks):
                b = q % 3
                a.wait_ge(d_xi[b], 16 * (q // 3 + 1))
                if q >= 3:
                    a.wait_ge(d_ro[b], 16 * (q // 3))
                a.activation(RB[:, b, 0:n, 16:24].bitcast(bf16), XI[:, b, 0:n, :], ACT.Copy).then_inc(S["a_hi"], 1)
                if q >= 1:
                    mid(q - 1)
                a.activation(RB[:, b, 0:n, 0:16].bitcast(f32), XI[:, b, 0:n, :], ACT.Copy).then_inc(S["a_fs"], 1)
                a.copy(RB[:, b, 0:n, 40:41], SR[:, o:o + n].unsqueeze(2)).then_inc(S["a_fs"], 1)
            mid(nq - 1)

            def expand(t):
                a.wait_ge(d_rec[t % 3], 16 * (t // 3 + 1))
                if t >= 2:
                    a.wait_ge(S["p_T"], t - 1)
                rec = REC[:, t % 3, :].rearrange("p (j w) -> p j w", w=RW)
                x = XP[:, t % 2, :, :]
                a.activation(x[:, :, 0:48], rec[:, :, 16:40].bitcast(bf16), ACT.Copy).then_inc(S["a_xp"], 1)
                a.activation(x[:, :, 48:80], rec[:, :, 16:32].bitcast(bf16), ACT.Copy).then_inc(S["a_xp"], 1)
                a.activation(x[:, :, 80:96], rec[:, :, 16:24].bitcast(bf16), ACT.Copy).then_inc(S["a_xp"], 1)
                a.activation(x[:, :, 99:100], FLG[:, t, :].unsqueeze(2), ACT.Copy).then_inc(S["a_xp"], 1)

            def evac(t):
                a.wait_ge(S["p_T"], t + 1)
                if t >= 2:
                    a.wait_ge(S["p_W"], 4 * (t - 2) + 4)
                a.activation(LT[:, t % 2, :], PTB[0:K, :], ACT.Copy).then_inc(S["a_T"], 1)

            def same(t):
                a.wait_ge(d_mk[t % 3], 16 * (t // 3 + 1))
                nid = MK[:, t % 3, 0:128]
                n = 4 * t - 2 if t else 0
                pairs = [(U, NID[:, t:t + 1])] + ([(CM, MK[:, (t - 1) % 3, 127:128])] if t else [])
                for k, (_, ref) in enumerate(pairs):
                    a.activation(UA[:, k, :], nid, ACT.Abs, bias=ref, scale=-1.0).then_inc(S["a_u"], 1)
                a.wait_ge(S["a_u"], n + len(pairs))
                for k, (to, _) in enumerate(pairs):
                    a.activation(to[:, t % 3, :], UA[:, k, :], ACT.Relu, bias=1.0, scale=-1.0).then_inc(S["a_u"], 1)
                a.wait_ge(S["a_u"], 4 * t + 2)

            def carried(t):
                a.wait_ge(S["p_X"], t)
                a.wait_ge(S["a_al"], t)
                for h in range(2):
                    a.activation(CC[:, h:4:2], PAL[:, h:4:2], ACT.Copy, scale=AL[:, t % 2, h:h + 1])\
                     .then_inc(S["a_c"], 1)
                a.wait_ge(S["a_c"], 6 * (t - 1) + 2)
                for q in range(4):
                    a.activation(DGM[:, q, :], IDN, ACT.Copy, scale=CC[:, q:q + 1]).then_inc(S["a_c"], 1)

            a.wait_ge(S["v_rb"], 3)
            a.wait_ge(S["g_m"], 8)
            expand(0)
            evac(0)
            expand(1)
            same(0)
            for t in range(NT + 1):
                if t + 1 < NT:
                    evac(t + 1)
                if t + 2 < NT:
                    expand(t + 2)
                if t + 1 < NT:
                    same(t + 1)
                if 1 <= t < NT:
                    a.wait_ge(S["v_scan"], 4 * t + 4)
                    if t >= 2:
                        a.wait_ge(S["a_al"], t - 1)
                        a.wait_ge(S["a_c"], 6 * (t - 2))
                    for h in range(2):
                        a.activation(DR[:, h:h + 1], MT[:, (t - 1) % 2, 128 * h + 127:128 * h + 128], ACT.Relu, scale=-1.0,
                                     bias=MT[:, t % 2, 128 * h:128 * h + 1]).then_inc(S["a_rel"], 1)
                    a.wait_ge(S["a_rel"], 2 * t)
                    a.activation(AL[:, t % 2, :], DR[:, :], ACT.Exp, scale=-1.0).then_inc(S["a_al"], 1)
                if t < NT:
                    a.wait_ge(S["p_S"], t + 1)
                    if t >= 4:
                        a.wait_ge(d_st[t % 4], 16 * (t // 4))
                    a.activation(DNS[:, t % 4, 512:528], PAL[:, 256:272], ACT.Copy).then_inc(S["a_sev"], 1)
                    a.wait_ge(S["a_sev"], t + 1)
                if t + 1 < NT:
                    a.activation(SE[:, t % 2, :], DNS[:, t % 4, 512:528], ACT.Copy, scale=E127).then_inc(S["a_se"], 1)
                if t < NT:
                    e = EM[:, t % 3, :].rearrange("p (x a o) -> p x a o", a=2, o=16)
                    a.wait_ge(S["v_sub"], t + 1)
                    for h in range(2):
                        v = e[:, 64 * h:64 * h + 64, 0, :]
                        a.activation(v, v, ACT.Exp).then_inc(S["a_exp"], 1)
                if t >= 2:
                    carried(t - 1)
                if t >= 1:
                    u = t - 1
                    a.wait_ge(S["p_sum"], u + 1)
                    if u >= 4:
                        a.wait_ge(d_st[u % 4], 16 * (u // 4))
                    a.activation(DNS[:, u % 4, 0:512], PDN[:, :], ACT.Copy).then_inc(S["a_dn"], 1)
            for g in range(NG):
                a.wait_ge(d_dt[g % 2], 16 * (g // 2 + 1))
                d = DTT[:, g % 2, :, 0:512].rearrange("p c (a i o) -> p c a i o", a=2, o=16)
                if g >= 1:
                    a.wait_ge(S["a_r"], 2 * g)
                a.activation(LN.rearrange("p (c i o) -> p c i o", i=16, o=16), d[:, :, 0, :, :], ACT.Ln).then_inc(S["a_r"], 1)
                a.activation(SA[:, GC * g:GC * g + GC, :], DTT[:, g % 2, :, 512:528], ACT.Copy).then_inc(S["a_sa"], 1)
                a.wait_ge(S["a_r"], 2 * g + 1)
                if g >= 1:
                    a.wait_ge(S["v_e"], 4 * (g - 1) + 3)
                a.activation(RR, LN, ACT.Exp, scale=-1.0).then_inc(S["a_r"], 1)
            for k in range(2):
                a.wait_ge(S["v_var"], k + 1)
                a.activation(ST[:, 2, :], ST[:, 1, :], ACT.Sqrt).then_inc(S["a_z"], 1)

        @block.tensor
        def _(pe):
            pe.wait_ge(S["d_cs"], 16)
            pe.wait_ge(S["v_p"], 1)
            pe.matmul(PMB[:, 0:NB], ONE, FF[:, :], start=True, stop=True).then_inc(S["p_f"], 1)
            pe.wait_ge(S["v_p"], 3)
            pe.matmul(PMB[:, 0:1], TRI, INC[:, NC - 1:NC], start=True, stop=True).then_inc(S["p_o"], 1)
            pe.wait_ge(S["v_p"], 4)
            pe.transpose(PMB[0:4, 0:128], F4[:, :, RC - 1], IDN).then_inc(S["p_x"], 1)
            pe.wait_ge(S["v_p"], 5)
            pe.transpose(PMB[:, 0:4], CX[:, 0:128], CS[0:4, 0:4]).then_inc(S["p_y"], 1)
            pe.wait_ge(S["v_tr"], 6)
            for h in range(2):
                for k, a in enumerate((TN[:, :, 1:129], TE, TC, TS)):
                    b = (PMB, PDN)[h]
                    pe.transpose(b[:, 128 * k:128 * k + 120], a[:, h, :], CS[0:120, 0:120]).then_inc(S["p_t"], 1)
            pe.wait_ge(S["d_w2"], 160)
            pe.wait_ge(S["v_id"], 1)

            def T(t):
                pe.wait_ge(S["a_xp"], 4 * t + 4)
                if t >= 1:
                    pe.wait_ge(S["a_T"], t)
                for j in range(L):
                    i = pe.transpose(PTB[0:K, 128 * j:128 * j + 128], XP[:, t % 2, j, :], IDB[:, :])
                i.then_inc(S["p_T"], 1)

            def W(t, k):
                if k == 0:
                    pe.wait_ge(S["a_T"], t + 1)
                m = 4 * t + k
                if m >= 2:
                    pe.wait_ge(S["v_mult"], m - 1)
                for j in (2 * k, 2 * k + 1):
                    i = pe.matmul(PW[:, j % 4, :], LT[:, t % 2, 128 * j:128 * j + 128], WS[:, :], start=True, stop=True)
                i.then_inc(S["p_W"], 1)

            def gsum(t, *slots):
                for j in slots:
                    if j == 0:
                        pe.wait_ge(S["v_gm"], 2 * t + 1)
                        if t >= 1:
                            pe.wait_ge(S["a_dn"], t)
                    if j == 4:
                        pe.wait_ge(S["v_gm"], 2 * t + 2)
                    last = t == 0 and j == L - 1
                    em = EM[:, t % 3, 512 * j:512 * j + 512].rearrange("p (i a o) -> p a i o", a=2, o=16)
                    i = pe.matmul(PDN[:, :], U[:, t % 3, :], em, start=(j == 0), stop=last)
                    if last:
                        i.then_inc(S["p_sum"], 1)

            def column(t):
                pe.wait_ge(S["a_dn"], t)
                pe.wait_ge(S["a_sev"], min(t + 2, NT))
                for q in range(4):
                    i = pe.matmul(PAL[:, q:q + 1], DNS[:, (t - 1) % 4, 128 * q:128 * q + 128], E127, start=True, stop=True)
                i.then_inc(S["p_X"], 1)

            def carry(t):
                if t >= 1:
                    pe.wait_ge(S["a_c"], 6 * t)
                    for q in range(4):
                        i = pe.matmul(PDN[:, 128 * q:128 * q + 128], CM[:, t % 3, :], DGM[:, q, :], start=False, stop=(q == 3))
                    i.then_inc(S["p_sum"], 1)

            pe.wait_ge(S["v_tr"], 14)
            T(0)
            W(0, 0)
            W(0, 1)
            for t in range(NT + 1):
                if t < NT:
                    W(t, 2)
                if t >= 2:
                    gsum(t - 2, 3)
                if t < NT:
                    W(t, 3)
                if t >= 2:
                    gsum(t - 2, 4, 5, 6, 7)
                    carry(t - 2)
                if t + 1 < NT:
                    T(t + 1)
                if t < NT:
                    pe.wait_ge(S["v_rmax"], t + 1)
                    pe.transpose(PMB[:, 0:128], MX[:, 0:128], IDN)
                    pe.transpose(PMB[:, 128:256], MX[:, 128:256], IDN).then_inc(S["p_mT"], 1)
                    pe.wait_ge(S["g_ev"], 3 * t + 3)
                    pe.wait_ge(S["a_u"], 4 * t + 2)
                    if t >= 1:
                        pe.wait_ge(S["a_sev"], t)
                    if t >= 3:
                        pe.wait_ge(S["a_c"], 6 * (t - 2))
                    for j in range(2):
                        i = pe.matmul(PAL[:, 256:272], U[:, t % 3, :], EQ[:, t % 2, j, :], start=(j == 0),
                                      stop=(t == 0 and j == 1))
                    if t >= 1:
                        pe.wait_ge(S["a_se"], t)
                        i = pe.matmul(PAL[:, 256:272], CM[:, t % 3, :], SE[:, (t - 1) % 2, :], start=False, stop=True)
                    i.then_inc(S["p_S"], 1)
                if t >= 1:
                    gsum(t - 1, 0)
                if t < NT:
                    pe.wait_ge(S["v_scan"], 4 * t + 4)
                    pe.transpose(PMB[:, 256:384], MT[:, t % 2, 0:128], IDN)
                    pe.transpose(PMB[:, 384:512], MT[:, t % 2, 128:256], IDN).then_inc(S["p_MB"], 1)
                if t >= 1:
                    gsum(t - 1, 1, 2)
                if t + 1 < NT:
                    W(t + 1, 0)
                    W(t + 1, 1)
                if t >= 2:
                    column(t - 1)
            gsum(NT - 1, 3, 4, 5, 6, 7)
            carry(NT - 1)

        @block.vector
        def _(v):
            chain = [0]
            lk = ctx.enter_context(nc.semaphore("v_link"))

            def link(i):
                chain[0] += 1
                i.then_inc(lk, 1)
                v.wait_ge(lk, chain[0])

            v.wait_ge(S["d_cs"], 16)
            v.tensor_copy(IDB[:, :], IDN).then_inc(S["v_id"], 1)
            v.wait_ge(S["d_f"], 16)
            v.tensor_copy(FF[:, :], FI[:, :]).then_inc(S["v_p"], 1)
            v.wait_ge(S["a_w"], 1)
            v.tensor_tensor(WD[:, :], WF[:, :], WH[:, 0, :], ALU.subtract).then_inc(S["v_w"], 1)
            v.wait_ge(S["a_w"], 2)
            v.tensor_tensor(WH[:, 2, :], WD[:, :], WH[:, 1, :], ALU.subtract).then_inc(S["v_w"], 1)

            def diff(q):
                n = chunks[q][1]
                v.wait_ge(S["a_hi"], q + 1)
                if q >= 2:
                    v.wait_ge(S["v_x3"], q - 1)
                v.tensor_tensor(XD[:, q % 2, 0:n, :], XI[:, q % 3, 0:n, :], RB[:, q % 3, 0:n, 16:24].bitcast(bf16),
                                ALU.subtract).then_inc(S["v_x1"], 1)

            def low(q):
                n = chunks[q][1]
                v.wait_ge(S["a_mid"], q + 1)
                v.tensor_tensor(RB[:, q % 3, 0:n, 32:40].bitcast(bf16), XD[:, q % 2, 0:n, :],
                                RB[:, q % 3, 0:n, 24:32].bitcast(bf16), ALU.subtract).then_inc(S["v_x3"], 1)

            def parts(n):
                for _ in range(n):
                    if done[0] < nq:
                        diff(done[0])
                    if 1 <= done[0] <= nq:
                        low(done[0] - 1)
                    done[0] += 1

            done = [0]
            v.wait_ge(S["p_f"], 1)
            link(v.tensor_copy(FB[:, :], PMB[:, 0:NB]))
            for g5 in range(5):
                for c in range(10 * g5, 10 * g5 + 10):
                    link(v.tensor_scalar(JK[:, 0:NB], FB[:, :], NVAL[:, c:c + 1], None, ALU.is_lt, ALU.add,
                                         accum_out=BC[:, c:c + 1]))
                s = slice(10 * g5, 10 * g5 + 10)
                link(v.tensor_scalar(QF[:, s], BC[:, s], 1.0, 0.0, ALU.subtract, ALU.max))
                v.tensor_copy(QI[:, s], QF[:, s]).then_inc(S["v_q"], 1)
                parts(1)
            for c in range(50):
                v.wait_ge(d_bl[c % 8], 16 * (c // 8 + 1))
                v.tensor_scalar(JK[:, :], BF[:, c % 8, :], NVAL[:, c:c + 1], None, ALU.is_lt, ALU.add,
                                accum_out=CB[:, c:c + 1]).then_inc(S["v_blk"], 1)
                v.wait_ge(S["v_blk"], c + 1)
                if c % 4 == 3:
                    parts(1)
            link(v.scalar_tensor_tensor(SS[:, :], QF[:, :], float(EB), CB[:, :], ALU.mult, ALU.add))
            link(v.tensor_tensor(DG[:, :], SS[:, 1:50], SS[:, 0:49], ALU.subtract))
            link(v.tensor_scalar(T1[:, :], DG[:, :], 7.0, None, ALU.add))
            link(v.tensor_copy(TI[:, :], T1[:, :]))
            link(v.tensor_scalar(TJ[:, :], TI[:, :], 3, None, ALU.logical_shift_right))
            link(v.tensor_copy(NRW[:, :], TJ[:, :]))
            v.wait_ge(S["g_m"], 8)
            i = v.tensor_tensor_scan(INC[:, :], NRW[:, :], ZR[:, 0:NC], 0.0, ALU.add, ALU.add)
            i.then_inc(S["v_p"], 2)
            v.wait_ge(S["v_p"], 3)
            link(v.tensor_tensor(T1[:, :], INC[:, :], NRW[:, :], ALU.subtract))
            v.wait_ge(S["p_o"], 1)
            link(v.tensor_copy(OFF[:, :], PMB[:, 0:1]))
            link(v.tensor_scalar(NV[:, :, 3], T1[:, :], OFF[:, 0:1], None, ALU.add))
            link(v.tensor_copy(NV[:, :, 0], NVAL[:, 0:NC]))
            link(v.tensor_copy(NV[:, :, 1], SS[:, 0:49]))
            link(v.tensor_copy(NV[:, :, 2], SS[:, 1:50]))
            link(v.tensor_scalar(T1[:, :], NRW[:, :], 0.0, NONE, ALU.is_equal, ALU.mult))
            v.tensor_tensor(SI[:, :], T1[:, :], NV[:, :, 3], ALU.add).then_inc(S["v_pc"], 1)
            parts(nq + 1 - done[0])
            v.wait_ge(S["d_rl"], 16)
            for f in range(4):
                i = v.tensor_tensor_scan(F4[:, f, :], RT[:, :, f], RT[:, :, f], -1.0, ALU.max, ALU.max)
                link(i)
            v.tensor_copy(CY[:, :], F4[:, :, RC - 1]).then_inc(S["v_p"], 1)
            v.wait_ge(S["p_x"], 1)
            link(v.tensor_copy(CT[:, :], PMB[0:4, 0:128]))
            v.tensor_tensor_scan(CX[:, 1:129], CT[:, :], CT[:, :], -1.0, ALU.max, ALU.max).then_inc(S["v_p"], 1)
            v.wait_ge(S["p_y"], 1)
            link(v.tensor_copy(CY[:, :], PMB[:, 0:4]))
            link(v.tensor_tensor(F5[:, :, :], F4[:, :, :], CY[:, :].unsqueeze(2).broadcast_to([128, 4, RC]), ALU.max))
            link(v.tensor_tensor(R1[:, :], RID, F5[:, 3, :], ALU.subtract))
            link(v.scalar_tensor_tensor(R2[:, :], R1[:, :], float(L), F5[:, 1, :], ALU.mult, ALU.add))
            link(v.tensor_tensor(R3[:, :], R2[:, :], F5[:, 2, :], ALU.is_ge))
            link(v.tensor_tensor(R1[:, :], F5[:, 2, :], R2[:, :], ALU.subtract))
            v.tensor_scalar(RCN[:, :], R1[:, :], float(L), 0.0, ALU.min, ALU.max).then_inc(S["v_rr"], 1)
            v.wait_ge(S["v_rr"], 1)
            link(v.scalar_tensor_tensor(R1[:, :], R3[:, :], -1.0, R2[:, :], ALU.mult, ALU.mult))
            v.tensor_tensor(RE[:, :], R2[:, :], R1[:, :], ALU.add).then_inc(S["v_rr"], 1)
            v.scalar_tensor_tensor(RN[:, :], R3[:, :], float(N), F5[:, 0, :], ALU.mult, ALU.max).then_inc(S["v_rr"], 1)
            v.wait_ge(S["d_tl"], 64)
            mk = MKT[:, :, :].rearrange("t h (k r) -> t h k r", k=3)
            v.tensor_copy(mk[:, :, 0, :], TN[:, :, 1:129]).then_inc(S["v_tr"], 1)
            v.tensor_tensor(mk[:, :, 1, :], TN[:, :, 1:129], TN[:, :, 0:128], ALU.not_equal).then_inc(S["v_tr"], 1)
            v.tensor_tensor(mk[:, :, 2, :], TN[:, :, 1:129], TN[:, :, 2:130], ALU.not_equal).then_inc(S["v_tr"], 1)
            v.wait_ge(S["v_tr"], 3)
            link(v.tensor_scalar(TS[:, :, :], mk[:, :, 2, :], -NONE, NONE, ALU.mult, ALU.add))
            v.wait_ge(S["v_tr"], 3)
            v.tensor_scalar(mk[:, :, 1, :], mk[:, :, 1, :], BIG, None, ALU.mult).then_inc(S["v_tr"], 1)
            v.tensor_scalar(mk[:, :, 2, :], mk[:, :, 2, :], BIG, None, ALU.mult).then_inc(S["v_tr"], 1)
            v.tensor_tensor(TS[:, :, :], TS[:, :, :], TN[:, :, 1:129], ALU.add).then_inc(S["v_tr"], 1)
            for h in range(2):
                v.wait_ge(S["p_t"], 4 * h + 4)
                b = (PMB, PDN)[h]
                for k, a in enumerate((NID, E0, CNT, SX)):
                    v.tensor_copy(a[:, 120 * h:120 * h + 120], b[:, 128 * k:128 * k + 120]).then_inc(S["v_tr"], 1)
            v.wait_ge(S["v_tr"], 14)
            link(v.tensor_tensor(INV[:, :, :], IO8.unsqueeze(1).broadcast_to([128, RC, L]),
                                 CNT[:, :].unsqueeze(2).broadcast_to([128, RC, L]), ALU.is_ge))
            v.tensor_scalar(VAL[:, :, :], INV[:, :, :], -1.0, 1.0, ALU.mult, ALU.add).then_inc(S["v_rb"], 1)
            v.tensor_scalar(INI[:, :, :], INV[:, :, :], float(N), None, ALU.mult).then_inc(S["v_rb"], 1)
            v.tensor_copy(FLG[:, :, :], INV[:, :, :]).then_inc(S["v_rb"], 1)

            for t in range(NT + 1):
                b, e = t % 3, t % 2
                if t < NT:
                    v.wait_ge(d_mk[b], 16 * (t // 3 + 1))
                    if t >= 3:
                        v.wait_ge(S["p_sum"], t - 2)
                    v.wait_ge(d_h[b], 128 * (t // 3 + 1))
                    for k in range(4):
                        v.wait_ge(S["p_W"], 4 * t + k + 1)
                        w = PW[:, 2 * (k % 2):2 * (k % 2) + 2, :].rearrange("p j (i c) -> p (j i) c", c=32)
                        hb = H[:, b, 32 * k:32 * k + 32].unsqueeze(2).broadcast_to([128, 32, 32])
                        v.tensor_tensor(EM[:, b, 1024 * k:1024 * k + 1024].rearrange("p (x c) -> p x c", c=32), w, hb,
                                        ALU.mult).then_inc(S["v_mult"], 1)
                    v.wait_ge(S["v_mult"], 4 * t + 4)
                    if t >= 1:
                        v.wait_ge(S["p_mT"], t)
                    em = EM[:, b, :].rearrange("p (j i a o) -> p i a o j", j=L, a=2, o=16)
                    v.tensor_reduce(MX[:, :].rearrange("p (i o) -> p i o", o=16), em[:, :, 0, :, :], AX.X, ALU.max)\
                        .then_inc(S["v_rmax"], 1)

                def gm(u, h):
                    v.wait_ge(S["a_exp"], 2 * u + h + 1)
                    x = EM[:, u % 3, 2048 * h:2048 * h + 2048].rearrange("p (x a o) -> p x a o", a=2, o=16)
                    v.tensor_tensor(x[:, :, 1, :], x[:, :, 1, :], x[:, :, 0, :], ALU.mult).then_inc(S["v_gm"], 1)

                if t >= 1:
                    gm(t - 1, 0)
                if t < NT:
                    v.wait_ge(S["p_mT"], t + 1)
                    for h in range(2):
                        s = slice(128 * h, 128 * h + 128)
                        init = BIG if t == 0 else MT[:, 1 - e, 128 * h + 127:128 * h + 128]
                        v.tensor_tensor_scan(MF[:, s], MK[:, b, 128:256], PMB[:, s], init, ALU.add, ALU.max)\
                            .then_inc(S["v_scan"], 1)
                    for h in range(2):
                        s = slice(128 * h, 128 * h + 128)
                        v.wait_ge(S["v_scan"], 4 * t + h + 1)
                        if t >= 2:
                            v.wait_ge(S["a_rel"], 2 * (t - 1))
                        v.tensor_tensor_scan(MT[:, e, s][:, ::-1], MK[:, b, 256:384][:, ::-1], MF[:, s][:, ::-1], BIG,
                                             ALU.add, ALU.max).then_inc(S["v_scan"], 1)
                if t >= 1:
                    gm(t - 1, 1)
                if t < NT:
                    v.wait_ge(S["p_MB"], t + 1)
                    x = EM[:, b, :].rearrange("p (j i a o) -> p j i a o", j=L, a=2, o=16)
                    mb = PMB[:, 256:512].rearrange("p (i o) -> p i o", o=16)
                    v.tensor_tensor(x[:, :, :, 0, :], x[:, :, :, 0, :], mb.unsqueeze(1).broadcast_to([128, L, 16, 16]),
                                    ALU.subtract).then_inc(S["v_sub"], 1)
            for g in range(NG):
                d = DTT[:, g % 2, :, 0:512].rearrange("p c (a i o) -> p c a i o", a=2, o=16)
                r4, t4 = (x.rearrange("p (c i o) -> p c i o", i=16, o=16) for x in (RR, TP[:, :]))
                v.wait_ge(d_dt[g % 2], 16 * (g // 2 + 1))
                v.wait_ge(S["a_r"], 2 * g + 2)
                if g >= 1:
                    v.wait_ge(S["v_e"], 4 * g)
                v.tensor_tensor(t4, d[:, :, 0, :, :], r4, ALU.mult).then_inc(S["v_e"], 1)
                v.wait_ge(S["v_e"], 4 * g + 1)
                v.scalar_tensor_tensor(TP[:, :], TP[:, :], 2.0, RR, ALU.subtract, ALU.mult).then_inc(S["v_e"], 1)
                v.wait_ge(S["v_e"], 4 * g + 2)
                v.tensor_tensor(t4, d[:, :, 1, :, :], t4, ALU.mult).then_inc(S["v_e"], 1)
                v.wait_ge(S["v_e"], 4 * g + 3)
                v.tensor_reduce(FT[:, GC * g:GC * g + GC, :], TP[:, :].rearrange("p (c i o) -> p c o i", i=16, o=16), AX.X,
                                ALU.add).then_inc(S["v_e"], 1)
            v.wait_ge(S["v_e"], 4 * NG)
            v.wait_ge(S["a_sa"], NG)
            v.wait_ge(S["d_xn"], 16)

            def bc(a):
                return a.unsqueeze(2).broadcast_to([128, NC, 16])

            def layernorm(k):
                link(v.tensor_reduce(ST[:, 0, :], Y[:, :, :], AX.X, ALU.add))
                link(v.tensor_scalar(ST[:, 3, :], ST[:, 0, :], 1.0 / 16, None, ALU.mult))
                link(v.tensor_tensor(XN[:, :, :], Y[:, :, :], bc(ST[:, 3, :]), ALU.subtract))
                link(v.tensor_tensor(Y2[:, :, :], XN[:, :, :], XN[:, :, :], ALU.mult))
                link(v.tensor_reduce(ST[:, 0, :], Y2[:, :, :], AX.X, ALU.add))
                v.tensor_scalar(ST[:, 1, :], ST[:, 0, :], 1.0 / 16, 1.0e-5, ALU.mult, ALU.add).then_inc(S["v_var"], 1)
                v.wait_ge(S["a_z"], k + 1)
                link(v.reciprocal(ST[:, 0, :], ST[:, 2, :]))
                return v.tensor_tensor(Y2[:, :, :], XN[:, :, :], bc(ST[:, 0, :]), ALU.mult)

            link(v.tensor_tensor(Y[:, :, :], XN[:, :, :], FT[:, :, :], ALU.subtract))
            link(layernorm(0))
            link(v.tensor_scalar(T1[:, :], DG[:, :], 1.0, None, ALU.max))
            link(v.reciprocal(RCN2[:, :], T1[:, :]))
            link(v.tensor_tensor(SA[:, :, :], SA[:, :, :], bc(RCN2[:, :]), ALU.mult))
            link(v.tensor_tensor(Y[:, :, :], SA[:, :, :], Y2[:, :, :], ALU.add))
            layernorm(1).then_inc(S["v_fin"], 1)


def kernel(**inputs):
    import numpy as np
    import concourse.bacc as bacc
    from concourse.bass_utils import run_bass_kernel_spmd as run

    x, ea = np.asarray(inputs["x"]), np.asarray(inputs["edge_attr_16"])
    src, dst = np.asarray(inputs["src"]), np.asarray(inputs["dst"])
    xt = np.concatenate([x, np.ones((N, 16), x.dtype)])
    eap = np.concatenate([ea, np.zeros((EP - E, 16), ea.dtype)])
    srcp = np.concatenate([src, np.zeros(EP - E, src.dtype)])
    dstp = np.concatenate([dst, np.full(NB * EB - E, 1 << 20, dst.dtype)])
    wa, wm = (np.asarray(inputs[f"L0_gnn_W_{k}"]).reshape(16, 16, 1, 16) for k in ("attn", "msg"))
    ba, bm = (np.asarray(inputs[f"L0_gnn_b_{k}"]).reshape(1, 16, 1, 16) for k in ("attn", "msg"))
    wc = np.concatenate([np.concatenate([wa, wm], 2), np.concatenate([ba, bm], 2)], 0).reshape(17, 512)
    cst = np.zeros((128, 692), np.float32)
    p = np.arange(128)
    cst[:, 0:128] = np.eye(128)
    cst[:, 128:256] = p[:, None] < p[None, :]
    cst[127, 256] = 1
    cst[:, 257:307] = p[:, None] * NC + np.arange(50)
    cst[:, 307:547] = p[:, None] * RC + np.arange(RC)
    cst[:, 547:555] = np.arange(8)
    cst[0, 555:557] = -1, -2
    cst[0, 557:685] = 1

    nc = bacc.Bacc("TRN2", target_bir_lowering=False, num_devices=1)
    arrays, args = {}, []
    for name, a in (("xt", xt), ("dst", dstp), ("src", srcp), ("ea", eap), ("wc", wc), ("cst", cst)):
        a = np.ascontiguousarray(a)
        arrays[f"in_{name}"] = a
        args.append(nc.dram_tensor(f"in_{name}", a.shape, mybir.dt.from_np(a.dtype), kind="ExternalInput").ap())
    o = nc.dram_tensor("out_0", (N, 16), mybir.dt.float32, kind="ExternalOutput").ap()
    gnn_kernel(nc, *args, o)
    r = run(nc, [arrays], core_ids=[0])
    return r.results[0]["out_0"]
```

```python
import concourse.bass as bass
from concourse import mybir
from contextlib import ExitStack

N = 6250
E = 200000
L = 8
NC = 49
NP = 128 * NC
EB = 512
NB = 391
EC = 1563
EP = 128 * EC
NT = 239
NS = 218
T0 = NS - 2
RC = 240
NR = 128 * RC
RW = 41
DW = 528
K = 100
BIG = -1.0e35
NONE = 100000.0
PADS = -1.0e25


def gnn_kernel(nc, xt, dst, src, ea, wc, cst, out):
    f32, bf16, i32 = mybir.dt.float32, mybir.dt.bfloat16, mybir.dt.int32
    ALU, ACT, AX = mybir.AluOpType, mybir.ActivationFunctionType, mybir.AxisListType
    RECD = nc.dram_tensor("rec_d", [EP, RW], i32, kind="Internal").ap()
    RTD = nc.dram_tensor("rt_d", [NR, 4], f32, kind="Internal").ap()
    NIDD = nc.dram_tensor("nid_d", [NR + 2], f32, kind="Internal").ap()
    E0D = nc.dram_tensor("e0_d", [NR], f32, kind="Internal").ap()
    CND = nc.dram_tensor("cn_d", [NR], f32, kind="Internal").ap()
    MKD = nc.dram_tensor("mk_d", [RC, 384], f32, kind="Internal").ap()
    DTD = nc.dram_tensor("dt_d", [NP, DW], f32, kind="Internal").ap()

    ctx = ExitStack()
    with ctx:
        def sb(name, shape, dt=f32):
            return ctx.enter_context(nc.sbuf_tensor(name, shape, dt))

        def sem(name):
            return ctx.enter_context(nc.semaphore(name))

        CS = sb("CS", [128, 692])
        IDN, TRI, E127 = CS[:, 0:128], CS[:, 128:256], CS[:, 256:257]
        NVAL, RID, IO8 = CS[:, 257:307], CS[:, 307:547], CS[:, 547:555]
        SENT, ONE = CS[0:1, 555:557], CS[0:1, 557:685]
        IDB = sb("IDB", [128, 128], bf16)
        FI = sb("FI", [1, NB], i32)
        FF = sb("FF", [1, NB])
        FB = sb("FB", [128, NB])
        JK = sb("JK", [128, 512])
        BC = sb("BC", [128, 50])
        QF = sb("QF", [128, 50])
        QI = sb("QI", [128, 50], i32)
        EM = sb("EM", [128, 3, L * 512])
        BF = EM[:, 1, :].rearrange("p (b e) -> p b e", b=8)
        CB = sb("CB", [128, 50])
        SS = sb("SS", [128, 50])
        DG = sb("DG", [128, NC])
        T1 = sb("T1", [128, NC])
        TI = sb("TI", [128, NC], i32)
        TJ = sb("TJ", [128, NC], i32)
        NRW = sb("NRW", [128, NC])
        INC = sb("INC", [128, NC])
        OFF = sb("OFF", [128, 1])
        NV = sb("NV", [128, NC, 4])
        TOT = sb("TOT", [1, 1], i32)
        SI = sb("SI", [128, NC], i32)
        SZ = sb("SZ", [128, NC], i32)
        ZR = sb("ZR", [128, RC])
        M1 = EM[:, 2, 0:960]
        RT = EM[:, 2, 960:1920].rearrange("p (c w) -> p c w", w=4)
        F4 = EM[:, 2, 1920:2880].rearrange("p (w c) -> p w c", w=4)
        F5 = EM[:, 2, 2880:3840].rearrange("p (w c) -> p w c", w=4)
        CX = sb("CX", [4, 132])
        CT = sb("CT", [4, 128])
        CY = sb("CY", [128, 4])
        R1 = sb("R1", [128, RC])
        R2 = sb("R2", [128, RC])
        R3 = sb("R3", [128, RC])
        RE = sb("RE", [128, RC])
        RCN = sb("RCN", [128, RC])
        RN = sb("RN", [128, RC])
        TN = sb("TN", [120, 2, 130])
        TE = sb("TE", [120, 2, 128])
        TC = sb("TC", [120, 2, 128])
        TS = sb("TS", [120, 2, 128])
        MKT = sb("MKT", [120, 2, 384])
        NID = sb("NID", [128, RC])
        E0 = sb("E0", [128, RC], i32)
        CNT = sb("CNT", [128, RC])
        SX = sb("SX", [128, RC], i32)
        INV = EM[:, 0, 2176:4096].rearrange("p (c j) -> p c j", j=L)
        VAL = sb("VAL", [128, RC, L])
        INI = sb("INI", [128, RC, L], i32)
        FLG = sb("FLG", [128, RC, L], bf16)
        DI = sb("DI", [128, DW])
        WF = sb("WF", [17, 512])
        WH = sb("WH", [17, 3, 512], bf16)
        WD = sb("WD", [17, 512])
        FLW = sb("FLW", [1, 512], bf16)
        WS = sb("WS", [K, 512], bf16)
        CH = 48
        chunks = [(o, min(CH, EC - o)) for o in range(0, EC, CH)]
        XI = EM[:, 0, 0:3 * CH * 16].rearrange("p (b c k) -> p b c k", b=3, k=16)
        SR = sb("SR", [128, EC], i32)
        XD = EM[:, 0, 3 * CH * 16:5 * CH * 16].rearrange("p (b c k) -> p b c k", b=2, k=16)
        RB = sb("RB", [128, 3, CH, RW], i32)
        REC = sb("REC", [128, 3, L * RW], i32)
        IX = sb("IX", [128, 3, L], i32)
        H = sb("H", [128, 3, L * 16])
        XP = sb("XP", [128, 2, L, K], bf16)
        LT = sb("LT", [K, 2, L * 128], bf16)
        MX = sb("MX", [128, 256])
        MF = sb("MF", [128, 256])
        MT = sb("MT", [128, 2, 256])
        MK = sb("MK", [128, 3, 384])
        U = sb("U", [128, 3, 128])
        CM = sb("CM", [128, 3, 128])
        UA = sb("UA", [128, 2, 128])
        DR = sb("DR", [128, 2])
        AL = sb("AL", [128, 2, 2])
        CC = sb("CC", [128, 4])
        DGM = sb("DGM", [128, 4, 128])
        SE = sb("SE", [128, 2, 16])
        DNS = sb("DNS", [128, 4, DW])
        EV = sb("EV", [128, 2, L, 16])
        EH = sb("EH", [128, 4, 16])
        EQ = sb("EQ", [128, 2, 2, 16])
        GC = 7
        NG = NC // GC
        DTT = EM[:, 0:2, 0:GC * DW].rearrange("p b (c w) -> p b c w", w=DW)
        LN = EM[:, 2, 0:256 * GC]
        RR = EM[:, 2, 256 * GC:512 * GC]
        TP = sb("TP", [128, 256 * GC])
        FT = sb("FT", [128, NC, 16])
        SA = sb("SA", [128, NC, 16])
        XN = sb("XN", [128, NC, 16])
        Y = sb("Y", [128, NC, 16])
        Y2 = sb("Y2", [128, NC, 16])
        ST = sb("ST", [128, 4, NC])
        RCN2 = sb("RCN2", [128, NC])

        PW = ctx.enter_context(nc.psum_tensor("PW", [128, 4, 512], f32))
        PTB = ctx.enter_context(nc.psum_tensor("PTB", [128, L * 128], bf16))
        PMB = ctx.enter_context(nc.psum_tensor("PMB", [128, 512], f32))
        PDN = ctx.enter_context(nc.psum_tensor("PDN", [128, 512], f32))
        PAL = ctx.enter_context(nc.psum_tensor("PAL", [128, 512], f32))

        names = """d_cs d_f d_w d_w2 d_sr d_i0 d_i1 d_sc0 d_rl d_s1 d_tl d_mkd d_out d_xn
            v_id v_p v_pc v_q v_blk v_rr v_tr v_rb v_w v_x1 v_x3
            v_mult v_rmax v_scan v_gm v_sub v_e v_var v_fin
            p_f p_o p_x p_y p_t p_T p_W p_mT p_S p_MB p_X p_sum
            a_w a_hi a_mid a_fs a_xp a_T a_exp a_rel a_al a_dn a_z a_sa a_u a_c a_se a_r a_sev a_m
            g_m g_idx g_ev""".split()
        S = {n: sem(n) for n in names}
        d_xi = [sem(f"d_xi{i}") for i in range(3)]
        d_ro = [sem(f"d_ro{i}") for i in range(3)]
        d_bl = [sem(f"d_bl{i}") for i in range(8)]
        d_rec = [sem(f"d_rec{i}") for i in range(3)]
        d_h = [sem(f"d_h{i}") for i in range(3)]
        d_mk = [sem(f"d_mk{i}") for i in range(3)]
        d_st = [sem(f"d_st{i}") for i in range(4)]
        d_dt = [sem(f"d_dt{i}") for i in range(2)]
        nq = len(chunks)

        def runs(eng, step, finish):
            for t in range(T0):
                step(t, NT)
            rows_of_all = eng.alloc_register(f"rows_{eng.engine.value}")
            eng.wait_ge(S["v_pc"], 1)
            eng.reg_load(rows_of_all, TOT[0:1, 0:1])
            with eng.If_lt(rows_of_all, 128 * NS + 1):
                for t in range(T0, NS + 1):
                    step(t, NS)
                finish(NS)
            with eng.Else():
                for t in range(T0, NT + 1):
                    step(t, NT)
                finish(NT)

        block = ctx.enter_context(nc.Block())

        @block.sync
        def _(sp):
            sp.dma_start(CS[:, :], cst).then_inc(S["d_cs"], 16)
            sp.dma_start(FI[:, :], dst.rearrange("(b e) -> e b", e=EB)[0:1, :],
                         allow_slow_non_contiguous=True).then_inc(S["d_f"], 16)
            sp.dma_start(WF[:, :], wc).then_inc(S["d_w"], 16)
            sp.dma_start(SR[:, :], src.rearrange("(p c) -> p c", c=EC)).then_inc(S["d_sr"], 16)
            eav = ea.rearrange("(p c) k -> p c k", c=EC)
            recv = RECD.rearrange("(p c) w -> p c w", c=EC)

            def load(q):
                o, n = chunks[q]
                if q >= 3:
                    sp.wait_ge(S["a_hi"], q - 2)
                    sp.wait_ge(S["a_fs"], 2 * (q - 3) + 2)
                    sp.wait_ge(S["v_x1"], q - 2)
                sp.dma_start(XI[:, q % 3, 0:n, :], eav[:, o:o + n, :]).then_inc(d_xi[q % 3], 16)

            for q in range(3):
                load(q)
            sp.wait_ge(S["a_w"], 2)
            sp.wait_ge(S["v_w"], 2)
            sp.wait_ge(S["g_m"], 8)
            for k, part in enumerate((0, 0, 0, 1, 1, 2)):
                sp.dma_start(WS[16 * k:16 * k + 16, :], WH[0:16, part, :]).then_inc(S["d_w2"], 16)
            for k in range(3):
                sp.dma_start(WS[96 + k:97 + k, :], WH[16:17, k, :]).then_inc(S["d_w2"], 16)
            sp.dma_start(WS[99:100, :], FLW[:, :]).then_inc(S["d_w2"], 16)
            sp.dma_start(RTD.rearrange("(p c) w -> p (c w)", c=RC), M1[:, :]).then_inc(S["d_i0"], 16)
            for q, (o, n) in enumerate(chunks):
                sp.wait_ge(S["a_mid"], q + 1)
                sp.wait_ge(S["a_fs"], 2 * q + 2)
                sp.wait_ge(S["v_x3"], q + 1)
                sp.dma_start(recv[:, o:o + n, :], RB[:, q % 3, 0:n, :]).then_inc(d_ro[q % 3], 16)
                if q + 3 < nq:
                    load(q + 3)
            sp.wait_ge(S["d_mkd"], 16)
            sp.dma_start(XN[:, :, :], xt[0:NP, :].rearrange("(p c) k -> p c k", c=NC)).then_inc(S["d_xn"], 16)

            def masks(t, nt):
                if t >= nt:
                    return
                if t >= 3:
                    sp.wait_ge(S["v_scan"], 4 * (t - 3) + 4)
                    sp.wait_ge(S["a_u"], 4 * (t - 2) + 2)
                sp.dma_start(MK[:, t % 3, :], MKD[t:t + 1, :].broadcast_to([128, 384])).then_inc(d_mk[t % 3], 16)

            def stored(nt):
                sp.wait_ge(S["d_i1"], 16 * NC)
                for b in range(4):
                    sp.wait_ge(d_st[b], 16 * len(range(b, nt, 4)))

            runs(sp, masks, stored)
            dtv = DTD.rearrange("(p c) w -> p c w", c=NC)
            for g in range(NG):
                if g >= 2:
                    sp.wait_ge(S["v_e"], 4 * (g - 2) + 3)
                    sp.wait_ge(S["a_sa"], g - 1)
                sp.dma_start(DTT[:, g % 2, :, :], dtv[:, GC * g:GC * g + GC, :]).then_inc(d_dt[g % 2], 16)
            sp.wait_ge(S["v_fin"], 1)
            sp.dma_start(out[0:127 * NC, :].rearrange("(p c) k -> p c k", c=NC), Y2[0:127, :, :]).then_inc(S["d_out"], 16)
            sp.dma_start(out[127 * NC:N, :].unsqueeze(0), Y2[127:128, 0:N - 127 * NC, :]).then_inc(S["d_out"], 16)
            sp.wait_ge(S["d_out"], 32)

        @block.gpsimd
        def _(g):
            g.memset(FLW[:, :], 0.0).then_inc(S["g_m"], 1)
            g.wait_ge(S["g_m"], 1)
            flv = FLW[:, :].rearrange("p (i a o) -> p i a o", a=2, o=16)
            g.memset(M1[:, :], -1.0).then_inc(S["g_m"], 1)
            g.memset(DI[:, :], 0.0).then_inc(S["g_m"], 1)
            g.wait_ge(S["g_m"], 3)
            g.memset(DI[:, 0:256], 1.0).then_inc(S["g_m"], 1)
            g.memset(flv[:, :, 0, :], PADS).then_inc(S["g_m"], 1)
            g.memset(ZR[:, :], 0.0).then_inc(S["g_m"], 1)
            g.memset(XP[:, :, :, 96:99], 1.0).then_inc(S["g_m"], 1)
            g.memset(CX[:, 0:1], -1.0).then_inc(S["g_m"], 1)
            dv = dst.rearrange("(b e) -> b e", e=EB)
            for c in range(50):
                g.wait_ge(S["v_q"], c // 5 + 1)
                if c >= 8:
                    g.wait_ge(S["v_blk"], c - 7)
                g.indirect_dma_start(BF[:, c % 8, :], None, dv,
                                     bass.IndirectOffsetOnAxis(ap=QI[:, c:c + 1], axis=0)).then_inc(d_bl[c % 8], 16)
            g.wait_ge(S["v_pc"], 1)
            g.wait_ge(S["d_i0"], 16)
            for c in range(NC):
                g.indirect_dma_start(RTD, bass.IndirectOffsetOnAxis(ap=SI[:, c:c + 1], axis=0), NV[:, c, :], None,
                                     bounds_check=NR - 1, oob_is_err=False).then_inc(S["d_sc0"], 16)
            g.wait_ge(S["d_sc0"], 16 * NC)
            g.dma_start(RT[:, :, :], RTD.rearrange("(p c) w -> p c w", c=RC)).then_inc(S["d_rl"], 16)
            g.wait_ge(S["v_rr"], 3)
            g.dma_start(E0D.rearrange("(p c) -> p c", c=RC), RE[:, :]).then_inc(S["d_s1"], 16)
            g.dma_start(CND.rearrange("(p c) -> p c", c=RC), RCN[:, :]).then_inc(S["d_s1"], 16)
            g.dma_start(NIDD[1:NR + 1].rearrange("(p c) -> p c", c=RC), RN[:, :]).then_inc(S["d_s1"], 16)
            g.dma_start(NIDD[0:1].unsqueeze(0), SENT[:, 0:1]).then_inc(S["d_s1"], 16)
            g.dma_start(NIDD[NR + 1:NR + 2].unsqueeze(0), SENT[:, 1:2]).then_inc(S["d_s1"], 16)
            g.wait_ge(S["d_s1"], 80)
            v0 = NIDD[0:NR].rearrange("(h t r) -> t h r", h=2, r=128)
            v1 = NIDD[2:NR + 2].rearrange("(h t r) -> t h r", h=2, r=128)
            g.dma_start(TN[:, :, 0:128], v0).then_inc(S["d_tl"], 16)
            g.dma_start(TN[:, :, 128:130], v1[:, :, 126:128]).then_inc(S["d_tl"], 16)
            g.dma_start(TE[:, :, :], E0D.rearrange("(h t r) -> t h r", h=2, r=128)).then_inc(S["d_tl"], 16)
            g.dma_start(TC[:, :, :], CND.rearrange("(h t r) -> t h r", h=2, r=128)).then_inc(S["d_tl"], 16)
            g.wait_ge(S["v_tr"], 6)
            g.dma_start(MKD.rearrange("(h t) r -> t h r", h=2), MKT[:, :, :]).then_inc(S["d_mkd"], 16)
            g.wait_ge(S["d_mkd"], 16)
            g.wait_ge(S["v_tr"], 14)
            for b in range(3):
                g.wait_ge(d_ro[b], 16 * len(range(b, nq, 3)))

            def rows(t):
                if t >= 3:
                    g.wait_ge(S["a_xp"], 4 * (t - 3) + 4)
                g.indirect_dma_start(REC[:, t % 3, :], None, RECD,
                                     bass.IndirectOffsetOnAxis(ap=E0[:, t:t + 1], axis=0)).then_inc(d_rec[t % 3], 16)

            def sums(t):
                g.wait_ge(S["a_dn"], t + 1)
                g.wait_ge(S["a_sev"], t + 1)
                g.indirect_dma_start(DTD, bass.IndirectOffsetOnAxis(ap=SX[:, t:t + 1], axis=0), DNS[:, t % 4, :], None,
                                     bounds_check=N - 1, oob_is_err=False).then_inc(d_st[t % 4], 16)

            def gathers(t, nt):
                if t >= nt:
                    return
                b = t % 3
                if t >= 2:
                    g.wait_ge(S["g_idx"], t - 1)
                    g.wait_ge(S["g_ev"], 3 * (t - 1))
                if t + 1 < nt:
                    rows(t + 1)
                g.wait_ge(d_rec[b], 16 * (t // 3 + 1))
                rec = REC[:, b, :].rearrange("p (j w) -> p j w", w=RW)
                if t == 0:
                    g.wait_ge(S["v_rb"], 1)
                if t >= 3:
                    g.wait_ge(d_h[b], 128 * (t // 3))
                g.tensor_tensor(IX[:, b, :].unsqueeze(2), rec[:, :, 40:41], INI[:, t, :].unsqueeze(2), ALU.add)\
                    .then_inc(S["g_idx"], 1)
                g.wait_ge(S["g_idx"], t + 1)
                if t >= 3:
                    g.wait_ge(S["v_mult"], 4 * (t - 3) + 4)
                    g.wait_ge(S["a_m"], t - 2)
                for j in range(L):
                    g.indirect_dma_start(H[:, b, 16 * j:16 * j + 16], None, xt,
                                         bass.IndirectOffsetOnAxis(ap=IX[:, b, j:j + 1], axis=0)).then_inc(d_h[b], 16)
                if t == 0:
                    g.wait_ge(S["v_rb"], 3)
                if t >= 2:
                    g.wait_ge(S["p_S"], t - 1)
                g.tensor_tensor(EV[:, t % 2, :, :], rec[:, :, 0:16].bitcast(f32),
                                VAL[:, t, :].unsqueeze(2).broadcast_to([128, L, 16]), ALU.mult).then_inc(S["g_ev"], 1)
                g.wait_ge(S["g_ev"], 3 * t + 1)
                g.tensor_tensor(EH[:, :, :], EV[:, t % 2, 0:4, :], EV[:, t % 2, 4:8, :], ALU.add).then_inc(S["g_ev"], 1)
                g.wait_ge(S["g_ev"], 3 * t + 2)
                g.tensor_tensor(EQ[:, t % 2, :, :], EH[:, 0:2, :], EH[:, 2:4, :], ALU.add).then_inc(S["g_ev"], 1)
                if t >= 3:
                    sums(t - 3)
                if t < NC:
                    g.indirect_dma_start(DTD, bass.IndirectOffsetOnAxis(ap=SZ[:, t:t + 1], axis=0), DI[:, :], None,
                                         bounds_check=NP - 1, oob_is_err=False).then_inc(S["d_i1"], 16)

            def stored(nt):
                for t in range(nt - 3, nt):
                    sums(t)
                for b in range(4):
                    g.wait_ge(d_st[b], 16 * len(range(b, nt, 4)))
                g.wait_ge(S["d_i1"], 16 * NC)

            rows(0)
            runs(g, gathers, stored)

        @block.scalar
        def _(a):
            a.wait_ge(S["d_w"], 16)
            a.activation(WH[:, 0, :], WF[:, :], ACT.Copy).then_inc(S["a_w"], 1)
            a.wait_ge(S["v_w"], 1)
            a.activation(WH[:, 1, :], WD[:, :], ACT.Copy).then_inc(S["a_w"], 1)

            a.wait_ge(S["d_sr"], 16)

            def mid(q):
                n = chunks[q][1]
                a.wait_ge(S["v_x1"], q + 1)
                a.activation(RB[:, q % 3, 0:n, 24:32].bitcast(bf16), XD[:, q % 2, 0:n, :], ACT.Copy).then_inc(S["a_mid"], 1)

            for q, (o, n) in enumerate(chunks):
                b = q % 3
                a.wait_ge(d_xi[b], 16 * (q // 3 + 1))
                if q >= 3:
                    a.wait_ge(d_ro[b], 16 * (q // 3))
                a.activation(RB[:, b, 0:n, 16:24].bitcast(bf16), XI[:, b, 0:n, :], ACT.Copy).then_inc(S["a_hi"], 1)
                if q >= 1:
                    mid(q - 1)
                a.activation(RB[:, b, 0:n, 0:16].bitcast(f32), XI[:, b, 0:n, :], ACT.Copy).then_inc(S["a_fs"], 1)
                a.copy(RB[:, b, 0:n, 40:41], SR[:, o:o + n].unsqueeze(2)).then_inc(S["a_fs"], 1)
            mid(nq - 1)

            def expand(t):
                a.wait_ge(d_rec[t % 3], 16 * (t // 3 + 1))
                if t >= 2:
                    a.wait_ge(S["p_T"], t - 1)
                rec = REC[:, t % 3, :].rearrange("p (j w) -> p j w", w=RW)
                x = XP[:, t % 2, :, :]
                a.activation(x[:, :, 0:48], rec[:, :, 16:40].bitcast(bf16), ACT.Copy).then_inc(S["a_xp"], 1)
                a.activation(x[:, :, 48:80], rec[:, :, 16:32].bitcast(bf16), ACT.Copy).then_inc(S["a_xp"], 1)
                a.activation(x[:, :, 80:96], rec[:, :, 16:24].bitcast(bf16), ACT.Copy).then_inc(S["a_xp"], 1)
                a.activation(x[:, :, 99:100], FLG[:, t, :].unsqueeze(2), ACT.Copy).then_inc(S["a_xp"], 1)

            def evac(t):
                a.wait_ge(S["p_T"], t + 1)
                if t >= 2:
                    a.wait_ge(S["p_W"], 4 * (t - 2) + 4)
                a.activation(LT[:, t % 2, :], PTB[0:K, :], ACT.Copy).then_inc(S["a_T"], 1)

            def same(t):
                a.wait_ge(d_mk[t % 3], 16 * (t // 3 + 1))
                nid = MK[:, t % 3, 0:128]
                n = 4 * t - 2 if t else 0
                pairs = [(U, NID[:, t:t + 1])] + ([(CM, MK[:, (t - 1) % 3, 127:128])] if t else [])
                for k, (_, ref) in enumerate(pairs):
                    a.activation(UA[:, k, :], nid, ACT.Abs, bias=ref, scale=-1.0).then_inc(S["a_u"], 1)
                a.wait_ge(S["a_u"], n + len(pairs))
                for k, (to, _) in enumerate(pairs):
                    a.activation(to[:, t % 3, :], UA[:, k, :], ACT.Relu, bias=1.0, scale=-1.0).then_inc(S["a_u"], 1)
                a.wait_ge(S["a_u"], 4 * t + 2)

            def carried(t):
                a.wait_ge(S["p_X"], t)
                a.wait_ge(S["a_al"], t)
                for h in range(2):
                    a.activation(CC[:, h:4:2], PAL[:, h:4:2], ACT.Copy, scale=AL[:, t % 2, h:h + 1])\
                     .then_inc(S["a_c"], 1)
                a.wait_ge(S["a_c"], 6 * (t - 1) + 2)
                for q in range(4):
                    a.activation(DGM[:, q, :], IDN, ACT.Copy, scale=CC[:, q:q + 1]).then_inc(S["a_c"], 1)

            a.wait_ge(S["v_rb"], 2)
            a.wait_ge(S["g_m"], 8)
            def product(t):
                a.wait_ge(d_h[t % 3], 128 * (t // 3 + 1))
                a.wait_ge(S["p_W"], 4 * t + 2)
                for i in range(16):
                    x = a.activation(EM[:, t % 3, 1536 + 32 * i:1568 + 32 * i], PW[:, 3, 32 * i:32 * i + 32], ACT.Copy,
                                     scale=H[:, t % 3, 48 + i:49 + i])
                x.then_inc(S["a_m"], 1)

            def weights(t, nt):
                if t + 1 < nt:
                    evac(t + 1)
                if t < nt:
                    a.wait_ge(S["p_S"], t + 1)
                    if t >= 4:
                        a.wait_ge(d_st[t % 4], 16 * (t // 4))
                    a.activation(DNS[:, t % 4, 512:528], PAL[:, 256:272], ACT.Copy).then_inc(S["a_sev"], 1)
                    a.wait_ge(S["a_sev"], t + 1)
                if t + 1 < nt:
                    a.activation(SE[:, t % 2, :], DNS[:, t % 4, 512:528], ACT.Copy, scale=E127).then_inc(S["a_se"], 1)
                if t + 1 < nt:
                    product(t + 1)
                if 1 <= t < nt:
                    a.wait_ge(S["v_scan"], 4 * t + 4)
                    if t >= 2:
                        a.wait_ge(S["a_al"], t - 1)
                        a.wait_ge(S["a_c"], 6 * (t - 2))
                    for h in range(2):
                        a.activation(DR[:, h:h + 1], MT[:, (t - 1) % 2, 128 * h + 127:128 * h + 128], ACT.Relu, scale=-1.0,
                                     bias=MT[:, t % 2, 128 * h:128 * h + 1]).then_inc(S["a_rel"], 1)
                    a.wait_ge(S["a_rel"], 2 * t)
                    a.activation(AL[:, t % 2, :], DR[:, :], ACT.Exp, scale=-1.0).then_inc(S["a_al"], 1)
                if t < nt:
                    e = EM[:, t % 3, :].rearrange("p (x a o) -> p x a o", a=2, o=16)
                    a.wait_ge(S["v_sub"], t + 1)
                    for h in range(2):
                        v = e[:, 64 * h:64 * h + 64, 0, :]
                        a.activation(v, v, ACT.Exp).then_inc(S["a_exp"], 1)
                if t >= 2:
                    carried(t - 1)
                if t + 2 < nt:
                    expand(t + 2)
                if t + 1 < nt:
                    same(t + 1)
                if t >= 1:
                    u = t - 1
                    a.wait_ge(S["p_sum"], u + 1)
                    if u >= 4:
                        a.wait_ge(d_st[u % 4], 16 * (u // 4))
                    a.activation(DNS[:, u % 4, 0:512], PDN[:, :], ACT.Copy).then_inc(S["a_dn"], 1)

            expand(0)
            evac(0)
            expand(1)
            same(0)
            product(0)
            runs(a, weights, lambda nt: None)
            for g in range(NG):
                a.wait_ge(d_dt[g % 2], 16 * (g // 2 + 1))
                d = DTT[:, g % 2, :, 0:512].rearrange("p c (a i o) -> p c a i o", a=2, o=16)
                if g >= 1:
                    a.wait_ge(S["a_r"], 2 * g)
                a.activation(LN.rearrange("p (c i o) -> p c i o", i=16, o=16), d[:, :, 0, :, :], ACT.Ln).then_inc(S["a_r"], 1)
                a.activation(SA[:, GC * g:GC * g + GC, :], DTT[:, g % 2, :, 512:528], ACT.Copy).then_inc(S["a_sa"], 1)
                a.wait_ge(S["a_r"], 2 * g + 1)
                if g >= 1:
                    a.wait_ge(S["v_e"], 4 * (g - 1) + 3)
                a.activation(RR, LN, ACT.Exp, scale=-1.0).then_inc(S["a_r"], 1)
            for k in range(2):
                a.wait_ge(S["v_var"], k + 1)
                a.activation(ST[:, 2, :], ST[:, 1, :], ACT.Sqrt).then_inc(S["a_z"], 1)

        @block.tensor
        def _(pe):
            pe.wait_ge(S["d_cs"], 16)
            pe.wait_ge(S["v_p"], 1)
            pe.matmul(PMB[:, 0:NB], ONE, FF[:, :], start=True, stop=True).then_inc(S["p_f"], 1)
            pe.wait_ge(S["v_p"], 3)
            pe.matmul(PMB[:, 0:1], TRI, INC[:, NC - 1:NC], start=True, stop=True)
            pe.wait_ge(S["g_m"], 8)
            pe.matmul(PMB[0:1, 1:2], INC[:, NC - 1:NC], DI[:, 0:1], start=True, stop=True).then_inc(S["p_o"], 1)
            pe.wait_ge(S["v_p"], 4)
            pe.transpose(PMB[0:4, 0:128], F4[:, :, RC - 1], IDN).then_inc(S["p_x"], 1)
            pe.wait_ge(S["v_p"], 5)
            pe.transpose(PMB[:, 0:4], CX[:, 0:128], CS[0:4, 0:4]).then_inc(S["p_y"], 1)
            pe.wait_ge(S["v_tr"], 6)
            for h in range(2):
                for k, a in enumerate((TN[:, :, 1:129], TE, TC, TS)):
                    b = (PMB, PDN)[h]
                    pe.transpose(b[:, 128 * k:128 * k + 120], a[:, h, :], CS[0:120, 0:120]).then_inc(S["p_t"], 1)
            pe.wait_ge(S["d_w2"], 160)
            pe.wait_ge(S["v_id"], 1)

            def T(t):
                pe.wait_ge(S["a_xp"], 4 * t + 4)
                if t >= 1:
                    pe.wait_ge(S["a_T"], t)
                for j in range(L):
                    i = pe.transpose(PTB[0:K, 128 * j:128 * j + 128], XP[:, t % 2, j, :], IDB[:, :])
                i.then_inc(S["p_T"], 1)

            def W(t, k):
                if k == 0:
                    pe.wait_ge(S["a_T"], t + 1)
                m = 4 * t + k
                if m >= 2:
                    pe.wait_ge(S["v_mult"], m - 1)
                if k == 3:
                    pe.wait_ge(S["a_m"], t + 1)
                for j in (2 * k, 2 * k + 1):
                    i = pe.matmul(PW[:, j % 4, :], LT[:, t % 2, 128 * j:128 * j + 128], WS[:, :], start=True, stop=True)
                i.then_inc(S["p_W"], 1)

            def gsum(t, *slots):
                for j in slots:
                    if j == 0:
                        pe.wait_ge(S["v_gm"], 2 * t + 1)
                        if t >= 1:
                            pe.wait_ge(S["a_dn"], t)
                    if j == 4:
                        pe.wait_ge(S["v_gm"], 2 * t + 2)
                    last = t == 0 and j == L - 1
                    em = EM[:, t % 3, 512 * j:512 * j + 512].rearrange("p (i a o) -> p a i o", a=2, o=16)
                    i = pe.matmul(PDN[:, :], U[:, t % 3, :], em, start=(j == 0), stop=last)
                    if last:
                        i.then_inc(S["p_sum"], 1)

            def column(t, nt):
                pe.wait_ge(S["a_dn"], t)
                pe.wait_ge(S["a_sev"], min(t + 2, nt))
                for q in range(4):
                    i = pe.matmul(PAL[:, q:q + 1], DNS[:, (t - 1) % 4, 128 * q:128 * q + 128], E127, start=True, stop=True)
                i.then_inc(S["p_X"], 1)

            def carry(t):
                if t >= 1:
                    pe.wait_ge(S["a_c"], 6 * t)
                    for q in range(4):
                        i = pe.matmul(PDN[:, 128 * q:128 * q + 128], CM[:, t % 3, :], DGM[:, q, :], start=False, stop=(q == 3))
                    i.then_inc(S["p_sum"], 1)

            def products(t, nt):
                if t < nt:
                    W(t, 2)
                if t < nt:
                    W(t, 3)
                if t >= 2:
                    gsum(t - 2, 4, 5, 6, 7)
                    carry(t - 2)
                if t + 1 < nt:
                    T(t + 1)
                if t < nt:
                    pe.wait_ge(S["v_rmax"], t + 1)
                    pe.transpose(PMB[:, 0:128], MX[:, 0:128], IDN)
                    pe.transpose(PMB[:, 128:256], MX[:, 128:256], IDN).then_inc(S["p_mT"], 1)
                    pe.wait_ge(S["g_ev"], 3 * t + 3)
                    pe.wait_ge(S["a_u"], 4 * t + 2)
                    if t >= 1:
                        pe.wait_ge(S["a_sev"], t)
                    if t >= 3:
                        pe.wait_ge(S["a_c"], 6 * (t - 2))
                    for j in range(2):
                        i = pe.matmul(PAL[:, 256:272], U[:, t % 3, :], EQ[:, t % 2, j, :], start=(j == 0),
                                      stop=(t == 0 and j == 1))
                    if t >= 1:
                        pe.wait_ge(S["a_se"], t)
                        i = pe.matmul(PAL[:, 256:272], CM[:, t % 3, :], SE[:, (t - 1) % 2, :], start=False, stop=True)
                    i.then_inc(S["p_S"], 1)
                if t + 1 < nt:
                    W(t + 1, 0)
                    W(t + 1, 1)
                if t < nt:
                    pe.wait_ge(S["v_scan"], 4 * t + 4)
                    pe.transpose(PMB[:, 256:384], MT[:, t % 2, 0:128], IDN)
                    pe.transpose(PMB[:, 384:512], MT[:, t % 2, 128:256], IDN).then_inc(S["p_MB"], 1)
                if t >= 1:
                    gsum(t - 1, 0, 1, 2, 3)
                if t >= 2:
                    column(t - 1, nt)

            def last(nt):
                gsum(nt - 1, 4, 5, 6, 7)
                carry(nt - 1)

            pe.wait_ge(S["v_tr"], 14)
            T(0)
            W(0, 0)
            W(0, 1)
            runs(pe, products, last)

        @block.vector
        def _(v):
            chain = [0]
            lk = ctx.enter_context(nc.semaphore("v_link"))

            def link(i):
                chain[0] += 1
                i.then_inc(lk, 1)
                v.wait_ge(lk, chain[0])

            v.wait_ge(S["d_cs"], 16)
            v.tensor_copy(IDB[:, :], IDN).then_inc(S["v_id"], 1)
            v.wait_ge(S["d_f"], 16)
            v.tensor_copy(FF[:, :], FI[:, :]).then_inc(S["v_p"], 1)
            v.wait_ge(S["a_w"], 1)
            v.tensor_tensor(WD[:, :], WF[:, :], WH[:, 0, :], ALU.subtract).then_inc(S["v_w"], 1)
            v.wait_ge(S["a_w"], 2)
            v.tensor_tensor(WH[:, 2, :], WD[:, :], WH[:, 1, :], ALU.subtract).then_inc(S["v_w"], 1)

            def diff(q):
                n = chunks[q][1]
                v.wait_ge(S["a_hi"], q + 1)
                if q >= 2:
                    v.wait_ge(S["v_x3"], q - 1)
                v.tensor_tensor(XD[:, q % 2, 0:n, :], XI[:, q % 3, 0:n, :], RB[:, q % 3, 0:n, 16:24].bitcast(bf16),
                                ALU.subtract).then_inc(S["v_x1"], 1)

            def low(q):
                n = chunks[q][1]
                v.wait_ge(S["a_mid"], q + 1)
                v.tensor_tensor(RB[:, q % 3, 0:n, 32:40].bitcast(bf16), XD[:, q % 2, 0:n, :],
                                RB[:, q % 3, 0:n, 24:32].bitcast(bf16), ALU.subtract).then_inc(S["v_x3"], 1)

            def parts(n):
                for _ in range(n):
                    if done[0] < nq:
                        diff(done[0])
                    if 1 <= done[0] <= nq:
                        low(done[0] - 1)
                    done[0] += 1

            done = [0]
            v.wait_ge(S["p_f"], 1)
            link(v.tensor_copy(FB[:, :], PMB[:, 0:NB]))
            for g5 in range(10):
                for c in range(5 * g5, 5 * g5 + 5):
                    link(v.tensor_scalar(JK[:, 0:NB], FB[:, :], NVAL[:, c:c + 1], None, ALU.is_lt, ALU.add,
                                         accum_out=BC[:, c:c + 1]))
                s = slice(5 * g5, 5 * g5 + 5)
                link(v.tensor_scalar(QF[:, s], BC[:, s], 1.0, 0.0, ALU.subtract, ALU.max))
                v.tensor_copy(QI[:, s], QF[:, s]).then_inc(S["v_q"], 1)
                if g5 in (0, 1, 3, 5, 7):
                    parts(1)
            for c in range(50):
                v.wait_ge(d_bl[c % 8], 16 * (c // 8 + 1))
                v.tensor_scalar(JK[:, :], BF[:, c % 8, :], NVAL[:, c:c + 1], None, ALU.is_lt, ALU.add,
                                accum_out=CB[:, c:c + 1]).then_inc(S["v_blk"], 1)
                v.wait_ge(S["v_blk"], c + 1)
                if c % 6 == 5:
                    parts(1)
            link(v.scalar_tensor_tensor(SS[:, :], QF[:, :], float(EB), CB[:, :], ALU.mult, ALU.add))
            link(v.tensor_tensor(DG[:, :], SS[:, 1:50], SS[:, 0:49], ALU.subtract))
            link(v.tensor_scalar(T1[:, :], DG[:, :], 7.0, None, ALU.add))
            link(v.tensor_copy(TI[:, :], T1[:, :]))
            link(v.tensor_scalar(TJ[:, :], TI[:, :], 3, None, ALU.logical_shift_right))
            link(v.tensor_copy(NRW[:, :], TJ[:, :]))
            v.wait_ge(S["g_m"], 8)
            i = v.tensor_tensor_scan(INC[:, :], NRW[:, :], ZR[:, 0:NC], 0.0, ALU.add, ALU.add)
            i.then_inc(S["v_p"], 2)
            v.wait_ge(S["v_p"], 3)
            link(v.tensor_tensor(T1[:, :], INC[:, :], NRW[:, :], ALU.subtract))
            v.wait_ge(S["p_o"], 1)
            link(v.tensor_copy(OFF[:, :], PMB[:, 0:1]))
            link(v.tensor_copy(TOT[:, :], PMB[0:1, 1:2]))
            link(v.tensor_scalar(NV[:, :, 3], T1[:, :], OFF[:, 0:1], None, ALU.add))
            link(v.tensor_copy(NV[:, :, 0], NVAL[:, 0:NC]))
            link(v.tensor_copy(NV[:, :, 1], SS[:, 0:49]))
            link(v.tensor_copy(NV[:, :, 2], SS[:, 1:50]))
            link(v.tensor_scalar(T1[:, :], NRW[:, :], 0.0, NONE, ALU.is_equal, ALU.mult))
            link(v.tensor_tensor(SI[:, :], T1[:, :], NV[:, :, 3], ALU.add))
            link(v.tensor_scalar(T1[:, :], DG[:, :], 0.0, NONE, ALU.not_equal, ALU.mult))
            v.tensor_tensor(SZ[:, :], T1[:, :], NVAL[:, 0:NC], ALU.add).then_inc(S["v_pc"], 1)
            parts(15)
            v.wait_ge(S["d_rl"], 16)
            for f in range(4):
                i = v.tensor_tensor_scan(F4[:, f, :], RT[:, :, f], RT[:, :, f], -1.0, ALU.max, ALU.max)
                link(i)
            v.tensor_copy(CY[:, :], F4[:, :, RC - 1]).then_inc(S["v_p"], 1)
            v.wait_ge(S["p_x"], 1)
            link(v.tensor_copy(CT[:, :], PMB[0:4, 0:128]))
            v.tensor_tensor_scan(CX[:, 1:129], CT[:, :], CT[:, :], -1.0, ALU.max, ALU.max).then_inc(S["v_p"], 1)
            v.wait_ge(S["p_y"], 1)
            link(v.tensor_copy(CY[:, :], PMB[:, 0:4]))
            link(v.tensor_tensor(F5[:, :, :], F4[:, :, :], CY[:, :].unsqueeze(2).broadcast_to([128, 4, RC]), ALU.max))
            link(v.tensor_tensor(R1[:, :], RID, F5[:, 3, :], ALU.subtract))
            link(v.scalar_tensor_tensor(R2[:, :], R1[:, :], float(L), F5[:, 1, :], ALU.mult, ALU.add))
            link(v.tensor_tensor(R3[:, :], R2[:, :], F5[:, 2, :], ALU.is_ge))
            link(v.tensor_tensor(R1[:, :], F5[:, 2, :], R2[:, :], ALU.subtract))
            v.tensor_scalar(RCN[:, :], R1[:, :], float(L), 0.0, ALU.min, ALU.max).then_inc(S["v_rr"], 1)
            v.wait_ge(S["v_rr"], 1)
            link(v.scalar_tensor_tensor(R1[:, :], R3[:, :], -1.0, R2[:, :], ALU.mult, ALU.mult))
            v.tensor_tensor(RE[:, :], R2[:, :], R1[:, :], ALU.add).then_inc(S["v_rr"], 1)
            v.scalar_tensor_tensor(RN[:, :], R3[:, :], float(N), F5[:, 0, :], ALU.mult, ALU.max).then_inc(S["v_rr"], 1)
            parts(nq + 1 - done[0])
            v.wait_ge(S["d_tl"], 64)
            mk = MKT[:, :, :].rearrange("t h (k r) -> t h k r", k=3)
            v.tensor_copy(mk[:, :, 0, :], TN[:, :, 1:129]).then_inc(S["v_tr"], 1)
            v.tensor_tensor(mk[:, :, 1, :], TN[:, :, 1:129], TN[:, :, 0:128], ALU.not_equal).then_inc(S["v_tr"], 1)
            v.tensor_tensor(mk[:, :, 2, :], TN[:, :, 1:129], TN[:, :, 2:130], ALU.not_equal).then_inc(S["v_tr"], 1)
            v.wait_ge(S["v_tr"], 3)
            link(v.tensor_scalar(TS[:, :, :], mk[:, :, 2, :], -NONE, NONE, ALU.mult, ALU.add))
            v.wait_ge(S["v_tr"], 3)
            v.tensor_scalar(mk[:, :, 1, :], mk[:, :, 1, :], BIG, None, ALU.mult).then_inc(S["v_tr"], 1)
            v.tensor_scalar(mk[:, :, 2, :], mk[:, :, 2, :], BIG, None, ALU.mult).then_inc(S["v_tr"], 1)
            v.tensor_tensor(TS[:, :, :], TS[:, :, :], TN[:, :, 1:129], ALU.add).then_inc(S["v_tr"], 1)
            for h in range(2):
                v.wait_ge(S["p_t"], 4 * h + 4)
                b = (PMB, PDN)[h]
                for k, a in enumerate((NID, E0, CNT, SX)):
                    v.tensor_copy(a[:, 120 * h:120 * h + 120], b[:, 128 * k:128 * k + 120]).then_inc(S["v_tr"], 1)
            v.wait_ge(S["v_tr"], 14)
            link(v.tensor_tensor(INV[:, :, :], IO8.unsqueeze(1).broadcast_to([128, RC, L]),
                                 CNT[:, :].unsqueeze(2).broadcast_to([128, RC, L]), ALU.is_ge))
            v.tensor_scalar(INI[:, :, :], INV[:, :, :], float(N), None, ALU.mult).then_inc(S["v_rb"], 1)
            v.tensor_copy(FLG[:, :, :], INV[:, :, :]).then_inc(S["v_rb"], 1)
            v.tensor_scalar(VAL[:, :, :], INV[:, :, :], -1.0, 1.0, ALU.mult, ALU.add).then_inc(S["v_rb"], 1)

            def scans(t, nt):
                b, e = t % 3, t % 2
                if t < nt:
                    v.wait_ge(d_mk[b], 16 * (t // 3 + 1))
                    if t >= 3:
                        v.wait_ge(S["p_sum"], t - 2)
                    v.wait_ge(d_h[b], 128 * (t // 3 + 1))
                    for k in range(4):
                        n = 1 if k == 1 else 2
                        if k == 2:
                            v.wait_ge(S["a_m"], t + 1)
                        v.wait_ge(S["p_W"], 4 * t + k + 1)
                        w = PW[:, 2 * (k % 2):2 * (k % 2) + n, :].rearrange("p j (i c) -> p (j i) c", c=32)
                        hb = H[:, b, 32 * k:32 * k + 16 * n].unsqueeze(2).broadcast_to([128, 16 * n, 32])
                        v.tensor_tensor(EM[:, b, 1024 * k:1024 * k + 512 * n].rearrange("p (x c) -> p x c", c=32), w, hb,
                                        ALU.mult).then_inc(S["v_mult"], 1)
                    v.wait_ge(S["v_mult"], 4 * t + 4)
                    if t >= 1:
                        v.wait_ge(S["p_mT"], t)
                    em = EM[:, b, :].rearrange("p (j i a o) -> p i a o j", j=L, a=2, o=16)
                    v.tensor_reduce(MX[:, :].rearrange("p (i o) -> p i o", o=16), em[:, :, 0, :, :], AX.X, ALU.max)\
                        .then_inc(S["v_rmax"], 1)

                def gm(u, h):
                    v.wait_ge(S["a_exp"], 2 * u + h + 1)
                    x = EM[:, u % 3, 2048 * h:2048 * h + 2048].rearrange("p (x a o) -> p x a o", a=2, o=16)
                    v.tensor_tensor(x[:, :, 1, :], x[:, :, 1, :], x[:, :, 0, :], ALU.mult).then_inc(S["v_gm"], 1)

                if t >= 1:
                    gm(t - 1, 0)
                if t < nt:
                    v.wait_ge(S["p_mT"], t + 1)
                    for h in range(2):
                        s = slice(128 * h, 128 * h + 128)
                        init = BIG if t == 0 else MT[:, 1 - e, 128 * h + 127:128 * h + 128]
                        v.tensor_tensor_scan(MF[:, s], MK[:, b, 128:256], PMB[:, s], init, ALU.add, ALU.max)\
                            .then_inc(S["v_scan"], 1)
                    for h in range(2):
                        s = slice(128 * h, 128 * h + 128)
                        v.wait_ge(S["v_scan"], 4 * t + h + 1)
                        if t >= 2:
                            v.wait_ge(S["a_rel"], 2 * (t - 1))
                        v.tensor_tensor_scan(MT[:, e, s][:, ::-1], MK[:, b, 256:384][:, ::-1], MF[:, s][:, ::-1], BIG,
                                             ALU.add, ALU.max).then_inc(S["v_scan"], 1)
                if t >= 1:
                    gm(t - 1, 1)
                if t < nt:
                    v.wait_ge(S["p_MB"], t + 1)
                    x = EM[:, b, :].rearrange("p (j i a o) -> p j i a o", j=L, a=2, o=16)
                    mb = PMB[:, 256:512].rearrange("p (i o) -> p i o", o=16)
                    v.tensor_tensor(x[:, :, :, 0, :], x[:, :, :, 0, :], mb.unsqueeze(1).broadcast_to([128, L, 16, 16]),
                                    ALU.subtract).then_inc(S["v_sub"], 1)

            runs(v, scans, lambda nt: None)
            for g in range(NG):
                d = DTT[:, g % 2, :, 0:512].rearrange("p c (a i o) -> p c a i o", a=2, o=16)
                r4, t4 = (x.rearrange("p (c i o) -> p c i o", i=16, o=16) for x in (RR, TP[:, :]))
                v.wait_ge(d_dt[g % 2], 16 * (g // 2 + 1))
                v.wait_ge(S["a_r"], 2 * g + 2)
                if g >= 1:
                    v.wait_ge(S["v_e"], 4 * g)
                v.tensor_tensor(t4, d[:, :, 0, :, :], r4, ALU.mult).then_inc(S["v_e"], 1)
                v.wait_ge(S["v_e"], 4 * g + 1)
                v.scalar_tensor_tensor(TP[:, :], TP[:, :], 2.0, RR, ALU.subtract, ALU.mult).then_inc(S["v_e"], 1)
                v.wait_ge(S["v_e"], 4 * g + 2)
                v.tensor_tensor(t4, d[:, :, 1, :, :], t4, ALU.mult).then_inc(S["v_e"], 1)
                v.wait_ge(S["v_e"], 4 * g + 3)
                v.tensor_reduce(FT[:, GC * g:GC * g + GC, :], TP[:, :].rearrange("p (c i o) -> p c o i", i=16, o=16), AX.X,
                                ALU.add).then_inc(S["v_e"], 1)
            v.wait_ge(S["v_e"], 4 * NG)
            v.wait_ge(S["a_sa"], NG)
            v.wait_ge(S["d_xn"], 16)

            def bc(a):
                return a.unsqueeze(2).broadcast_to([128, NC, 16])

            def layernorm(k):
                link(v.tensor_reduce(ST[:, 0, :], Y[:, :, :], AX.X, ALU.add))
                link(v.tensor_scalar(ST[:, 3, :], ST[:, 0, :], 1.0 / 16, None, ALU.mult))
                link(v.tensor_tensor(XN[:, :, :], Y[:, :, :], bc(ST[:, 3, :]), ALU.subtract))
                link(v.tensor_tensor(Y2[:, :, :], XN[:, :, :], XN[:, :, :], ALU.mult))
                link(v.tensor_reduce(ST[:, 0, :], Y2[:, :, :], AX.X, ALU.add))
                v.tensor_scalar(ST[:, 1, :], ST[:, 0, :], 1.0 / 16, 1.0e-5, ALU.mult, ALU.add).then_inc(S["v_var"], 1)
                v.wait_ge(S["a_z"], k + 1)
                link(v.reciprocal(ST[:, 0, :], ST[:, 2, :]))
                return v.tensor_tensor(Y2[:, :, :], XN[:, :, :], bc(ST[:, 0, :]), ALU.mult)

            link(v.tensor_tensor(Y[:, :, :], XN[:, :, :], FT[:, :, :], ALU.subtract))
            link(layernorm(0))
            link(v.tensor_scalar(T1[:, :], DG[:, :], 1.0, None, ALU.max))
            link(v.reciprocal(RCN2[:, :], T1[:, :]))
            link(v.tensor_tensor(SA[:, :, :], SA[:, :, :], bc(RCN2[:, :]), ALU.mult))
            link(v.tensor_tensor(Y[:, :, :], SA[:, :, :], Y2[:, :, :], ALU.add))
            layernorm(1).then_inc(S["v_fin"], 1)


def kernel(**inputs):
    import numpy as np
    import concourse.bacc as bacc
    from concourse.bass_utils import run_bass_kernel_spmd as run

    x, ea = np.asarray(inputs["x"]), np.asarray(inputs["edge_attr_16"])
    src, dst = np.asarray(inputs["src"]), np.asarray(inputs["dst"])
    xt = np.concatenate([x, np.ones((N, 16), x.dtype)])
    eap = np.concatenate([ea, np.zeros((EP - E, 16), ea.dtype)])
    srcp = np.concatenate([src, np.zeros(EP - E, src.dtype)])
    dstp = np.concatenate([dst, np.full(NB * EB - E, 1 << 20, dst.dtype)])
    wa, wm = (np.asarray(inputs[f"L0_gnn_W_{k}"]).reshape(16, 16, 1, 16) for k in ("attn", "msg"))
    ba, bm = (np.asarray(inputs[f"L0_gnn_b_{k}"]).reshape(1, 16, 1, 16) for k in ("attn", "msg"))
    wc = np.concatenate([np.concatenate([wa, wm], 2), np.concatenate([ba, bm], 2)], 0).reshape(17, 512)
    cst = np.zeros((128, 692), np.float32)
    p = np.arange(128)
    cst[:, 0:128] = np.eye(128)
    cst[:, 128:256] = p[:, None] < p[None, :]
    cst[127, 256] = 1
    cst[:, 257:307] = p[:, None] * NC + np.arange(50)
    cst[:, 307:547] = p[:, None] * RC + np.arange(RC)
    cst[:, 547:555] = np.arange(8)
    cst[0, 555:557] = -1, -2
    cst[0, 557:685] = 1

    nc = bacc.Bacc("TRN2", target_bir_lowering=False, num_devices=1)
    arrays, args = {}, []
    for name, a in (("xt", xt), ("dst", dstp), ("src", srcp), ("ea", eap), ("wc", wc), ("cst", cst)):
        a = np.ascontiguousarray(a)
        arrays[f"in_{name}"] = a
        args.append(nc.dram_tensor(f"in_{name}", a.shape, mybir.dt.from_np(a.dtype), kind="ExternalInput").ap())
    o = nc.dram_tensor("out_0", (N, 16), mybir.dt.float32, kind="ExternalOutput").ap()
    gnn_kernel(nc, *args, o)
    r = run(nc, [arrays], core_ids=[0])
    return r.results[0]["out_0"]
```
